# Optimizing a Trainium2 kernel written in Bass

```python
import numpy as np
import jax
import jax.numpy as jnp

def _softmax(x, axis=-1):
    return jax.nn.softmax(x, axis=axis)

def _gelu(x):
    return jax.nn.gelu(x, approximate=True)

def _silu(x):
    return jax.nn.silu(x)

def _sigmoid(x):
    return jax.nn.sigmoid(x)

def _layernorm(x, axis=-1, eps=1e-05):
    m = jnp.mean(x, axis=axis, keepdims=True)
    v = jnp.var(x, axis=axis, keepdims=True)
    return (x - m) / jnp.sqrt(v + eps)

def _scatter_add(tgt, idx, src, axis=0):
    return tgt.at[idx].add(src)

def _segment_sum(src, seg, n):
    return jax.ops.segment_sum(src, seg, n)
kernel_name = 'mk_xattn_ffn_d1_seqx_r8_799e19'

def setup_inputs(seed: int=0):
    np.random.seed(seed)
    _w = jnp.asarray

    def _rec_inputs():
        import jax
        import jax.numpy as jnp
        _rk = jax.random.key(seed)
        x = -0.0002928 + 1 * jax.random.normal(jax.random.fold_in(_rk, 1), (32, 64, 256), jnp.float32)
        _lenS = 64 - jax.random.randint(jax.random.fold_in(_rk, 7), (32,), 0, max(1, 64 // 4) + 1, jnp.int32)
        _lenS2 = 64 - jax.random.randint(jax.random.fold_in(_rk, 8), (32,), 0, max(1, 64 // 4) + 1, jnp.int32)
        _ctx_2048P = jax.random.normal(jax.random.fold_in(_rk, 11), (32, 16, 256), jnp.float32)
        _ctx_2048c = jax.random.dirichlet(jax.random.fold_in(_rk, 511), 0.3 * jnp.ones((16,), jnp.float32), (32, 64))
        _ctx_2048t = jnp.einsum('bsk,bkd->bsd', _ctx_2048c, _ctx_2048P)
        _ctx_2048t = _ctx_2048t * jax.lax.rsqrt(jnp.mean(jnp.square(_ctx_2048t)) + 1e-12) * 0.953939
        ctx_2048 = -1.39393e-06 + 0.999914 * (_ctx_2048t + 0.3 * jax.random.normal(jax.random.fold_in(_rk, 611), (32, 64, 256), jnp.float32))
        return (x, ctx_2048)
    x, ctx_2048 = _rec_inputs()

    def _L0_xattn_setup():
        import math
        import jax, jax.numpy as jnp
        import numpy as np
        N_HEADS = 8
        CHANNELS = 64
        K_CH = CHANNELS // N_HEADS
        THETA = 10000.0

        def _rope_freqs(length, dim):
            inv_freq = 1.0 / THETA ** (jnp.arange(0, dim, 2, dtype=jnp.float32) / dim)
            f = jnp.arange(length, dtype=jnp.float32)[:, None] * inv_freq[None, :]
            return jnp.concatenate([f, f], axis=-1)

        def _apply_rotary(pos, t):
            half = t.shape[-1] // 2
            rot = jnp.concatenate([-t[..., half:], t[..., :half]], axis=-1)
            return t * jnp.cos(pos) + rot * jnp.sin(pos)

        def _proj(inp, W, b):
            return jnp.einsum('oc,bct->bot', W, inp) + b[None, :, None]
        key = jax.random.key(seed)
        ks = jax.random.split(key, 10)
        B, C, T = (4, CHANNELS, 256)
        bound = math.sqrt(6.0 / (C + C))

        def w(k):
            return jax.random.uniform(k, (C, C), jnp.float32, -bound, bound)
        return {'x': jax.random.normal(ks[0], (B, C, T), jnp.float32), 'c': jax.random.normal(ks[1], (B, C, T), jnp.float32), 'Wq': w(ks[2]), 'bq': jnp.zeros((C,), jnp.float32), 'Wk': w(ks[3]), 'bk': jnp.zeros((C,), jnp.float32), 'Wv': w(ks[4]), 'bv': jnp.zeros((C,), jnp.float32), 'Wo': w(ks[5]), 'bo': jnp.zeros((C,), jnp.float32)}
    _L0_xattn_all = _L0_xattn_setup()
    _L0_xattn_in = {k: v for k, v in _L0_xattn_all.items() if k in ('Wq', 'bq', 'Wk', 'bk', 'Wv', 'bv', 'Wo', 'bo')}
    del _L0_xattn_all

    def _L0_ffn_setup():
        import jax, jax.numpy as jnp
        import numpy as np
        B, S, D, H = (8, 512, 256, 640)

        def ternarize_weight(w):
            abs_mean = jnp.maximum(jnp.mean(jnp.abs(w)), 1e-05)
            thr = 0.7 * abs_mean
            one = jnp.ones((), dtype=w.dtype)
            q = jnp.where(w > thr, one, jnp.where(w < -thr, -one, jnp.zeros((), dtype=w.dtype)))
            return w + jax.lax.stop_gradient(q * abs_mean - w)
        key = jax.random.key(seed)
        k1, k2, k3 = jax.random.split(key, 3)
        x = jax.random.normal(k1, (B, S, D), dtype=jnp.float32)
        w_fc = jax.random.normal(k2, (H, D), dtype=jnp.float32) / np.sqrt(D).astype(np.float32)
        w_proj = jax.random.normal(k3, (D, H), dtype=jnp.float32) / np.sqrt(H).astype(np.float32)
        return {'x': x, 'w_fc': w_fc, 'w_proj': w_proj}
    _L0_ffn_all = _L0_ffn_setup()
    _L0_ffn_in = {k: v for k, v in _L0_ffn_all.items() if k in ('w_fc', 'w_proj')}
    del _L0_ffn_all
    return {'x': x, 'ctx_2048': ctx_2048, 'L0_xattn_Wq': _L0_xattn_in['Wq'], 'L0_xattn_bq': _L0_xattn_in['bq'], 'L0_xattn_Wk': _L0_xattn_in['Wk'], 'L0_xattn_bk': _L0_xattn_in['bk'], 'L0_xattn_Wv': _L0_xattn_in['Wv'], 'L0_xattn_bv': _L0_xattn_in['bv'], 'L0_xattn_Wo': _L0_xattn_in['Wo'], 'L0_xattn_bo': _L0_xattn_in['bo'], 'L0_ffn_w_fc': _L0_ffn_in['w_fc'], 'L0_ffn_w_proj': _L0_ffn_in['w_proj']}

def reference(x, ctx_2048, L0_xattn_Wq, L0_xattn_bq, L0_xattn_Wk, L0_xattn_bk, L0_xattn_Wv, L0_xattn_bv, L0_xattn_Wo, L0_xattn_bo, L0_ffn_w_fc, L0_ffn_w_proj):
    import jax
    import jax.numpy as jnp

    def _L0_xattn_ref(x, c, Wq, bq, Wk, bk, Wv, bv, Wo, bo):
        import math
        import jax, jax.numpy as jnp
        import numpy as np
        N_HEADS = 8
        CHANNELS = 64
        K_CH = CHANNELS // N_HEADS
        THETA = 10000.0

        def _rope_freqs(length, dim):
            inv_freq = 1.0 / THETA ** (jnp.arange(0, dim, 2, dtype=jnp.float32) / dim)
            f = jnp.arange(length, dtype=jnp.float32)[:, None] * inv_freq[None, :]
            return jnp.concatenate([f, f], axis=-1)

        def _apply_rotary(pos, t):
            half = t.shape[-1] // 2
            rot = jnp.concatenate([-t[..., half:], t[..., :half]], axis=-1)
            return t * jnp.cos(pos) + rot * jnp.sin(pos)

        def _proj(inp, W, b):
            return jnp.einsum('oc,bct->bot', W, inp) + b[None, :, None]
        b, _, t_t = x.shape
        t_s = c.shape[2]
        q_emb = _rope_freqs(t_t, K_CH)
        k_emb = _rope_freqs(t_s, K_CH)

        def split_heads(t):
            return t.reshape(b, N_HEADS, K_CH, t.shape[2]).transpose(0, 1, 3, 2)
        q = split_heads(_proj(x, Wq, bq))
        k = split_heads(_proj(c, Wk, bk))
        v = split_heads(_proj(c, Wv, bv))
        q = _apply_rotary(q_emb, q)
        k = _apply_rotary(k_emb, k)
        scores = jnp.einsum('bhtc,bhsc->bhts', q, k) / math.sqrt(K_CH)
        p_attn = jax.nn.softmax(scores, axis=-1)
        out = jnp.einsum('bhts,bhsc->bhtc', p_attn, v)
        out = out.transpose(0, 1, 3, 2).reshape(b, N_HEADS * K_CH, t_t)
        return _proj(out, Wo, bo)

    def _L0_ffn_ref(x, w_fc, w_proj):
        import jax, jax.numpy as jnp
        import numpy as np
        B, S, D, H = (8, 512, 256, 640)

        def ternarize_weight(w):
            abs_mean = jnp.maximum(jnp.mean(jnp.abs(w)), 1e-05)
            thr = 0.7 * abs_mean
            one = jnp.ones((), dtype=w.dtype)
            q = jnp.where(w > thr, one, jnp.where(w < -thr, -one, jnp.zeros((), dtype=w.dtype)))
            return w + jax.lax.stop_gradient(q * abs_mean - w)
        h = jnp.einsum('bsd,hd->bsh', x, ternarize_weight(w_fc))
        h = jnp.square(jax.nn.relu(h))
        return jnp.einsum('bsh,dh->bsd', h, ternarize_weight(w_proj))
    x = x + _L0_xattn_ref(_layernorm(x, axis=-1), ctx_2048, L0_xattn_Wq, L0_xattn_bq, L0_xattn_Wk, L0_xattn_bk, L0_xattn_Wv, L0_xattn_bv, L0_xattn_Wo, L0_xattn_bo)
    x = x + _L0_ffn_ref(_layernorm(x, axis=-1), L0_ffn_w_fc, L0_ffn_w_proj)
    return x

_drawn_inputs = setup_inputs


def setup_inputs(seed=0):
    import zlib

    import numpy as np

    out = dict(_drawn_inputs(seed))
    spreads = {'L0_xattn_bq': (0.0, 0.286),
     'L0_xattn_bk': (0.0, 0.8),
     'L0_xattn_bv': (0.0, 0.1),
     'L0_xattn_bo': (0.0, 0.1)}
    factors = {}
    for name, (base, spread) in spreads.items():
        noise = np.random.default_rng([zlib.crc32(name.encode()), seed]).standard_normal(out[name].shape)
        drawn = base * np.exp(spread * noise) if base else spread * noise
        out[name] = jnp.asarray(drawn.astype(out[name].dtype))
    for name, factor in factors.items():
        out[name] = (out[name] * factor).astype(out[name].dtype)
    return out
```

```python
from contextlib import ExitStack

import concourse.bass as bass
from concourse import mybir

F32 = mybir.dt.float32
BF16 = mybir.dt.bfloat16
F16 = mybir.dt.float16
ALU = mybir.AluOpType
ACT = mybir.ActivationFunctionType
AX_X = mybir.AxisListType.X

BATCHES, C, T = 32, 64, 256
HEADS = 8
KC = C // HEADS
HID = 640
PAIRS = BATCHES // 2
P = 128
G = 2 * HEADS
TT = T // P
HT = HID // P
PARTS = 3
ROWS = PARTS * PARTS * KC
MROWS = ROWS + PARTS
RING = 3
EPS = 1e-5
RELU_SCALE = 1.0 / 16.0
SCALE = float(KC) ** -0.5

ORDER = [0, 2, 4, 6, 1, 3, 5, 7]

SMALL = [
    [("max1", 3), ("xT", 5), ("v", 2), ("att1", 4), ("back", 4), ("wo", 4), ("att0", 3)],
    [("k", 0), ("q", 0), ("hid0", 5), ("hid1", 5), ("hid2", 5), ("max0", 2), ("ffn2", 5)],
]
FIRST_FULL, LOOP_STEPS = 6, 9
STEPS = PAIRS + 6


class Count:

    def __init__(self, j, c):
        self.j, self.c = j, c

    def back(self, d):
        return Count(self.j, self.c - d)

    @property
    def real(self):
        return not isinstance(self.j, int) or 0 <= self.c < PAIRS

    @property
    def slot(self):
        return self.c % RING

    def times(self, k, more):
        fixed = self.c * k + more
        return fixed if isinstance(self.j, int) else self.j * (RING * k) + fixed

    def turns(self, k, more=0):
        fixed = (self.c // RING + 1) * k + more
        return fixed if isinstance(self.j, int) else self.j * k + fixed


def small_before(which, user, s):
    users = SMALL[which]
    at = [u for u, _ in users].index(user)
    if not isinstance(s.j, int):
        first = sum(0 <= t - lag < PAIRS for t in range(s.c) for _, lag in users)
        return s.j * (RING * len(users)) + (first + at)
    done = sum(0 <= t - lag < PAIRS for t in range(s.c) for _, lag in users)
    return done + sum(0 <= s.c - lag < PAIRS for _, lag in users[:at])


def run_steps(engine, step):
    for c in range(FIRST_FULL):
        step(Count(0, c))
    with engine.Fori(0, LOOP_STEPS // RING, 1) as j:
        for u in range(RING):
            step(Count(j, FIRST_FULL + u))
    for c in range(FIRST_FULL + LOOP_STEPS, STEPS):
        step(Count(0, c))


def xattn_ffn(nc, x, ctx_in, wq_bd, wk_bd, wv_bd, wo_bd, bq_col, bk_col, bv_col, bo_col, wfc_t, wproj_t,
              cos_t, sin_t, ident_t, out):
    with ExitStack() as ctx:
        def sb(name, shape, dt):
            return ctx.enter_context(nc.sbuf_tensor(name, shape, dt))

        def psum(name, shape, dt):
            return ctx.enter_context(nc.psum_tensor(name, shape, dt))

        def sem(name):
            return ctx.enter_context(nc.semaphore(name))

        spread = nc.dram_tensor("spread", [RING, 2, PARTS, P, T], BF16, kind="Internal").ap()

        wq = sb("wq", [P, P], F32)
        wk = sb("wk", [P, P], F32)
        wv = sb("wv", [P, P], F32)
        wo = sb("wo", [P, P], F32)
        bq = sb("bq", [P, 1], F32)
        bk = sb("bk", [P, 1], F32)
        bv = sb("bv", [P, 1], F32)
        bo = sb("bo", [P, 1], F32)
        out_bias = sb("out_bias", [P, 1], F32)
        cos = sb("cos", [P, T], F32)
        sin = sb("sin", [P, T], F32)
        ident = sb("ident", [P, P], F32)
        ident16 = sb("ident16", [P, P], BF16)
        ones = sb("ones", [P, P], F32)
        minus_half = sb("minus_half", [P, 1], F32)
        wfc = sb("wfc", [P, TT, HID], F32)
        wproj = sb("wproj", [P, HT, T], F32)
        below = sb("below", [P, 1280], F16)
        fc3 = sb("fc3", [P, TT, HID], F16)
        proj3 = sb("proj3", [P, HT, T], F16)
        wsum = sb("wsum", [P, 2], F32)
        wmean = sb("wmean", [P, 2], F32)
        wthr = sb("wthr", [P, 2], F32)
        wnthr = sb("wnthr", [P, 2], F32)
        fscale = sb("fscale", [P, 2], F32)

        xin = sb("xin", [P, RING, T], F32)
        cin = sb("cin", [P, RING, T], F32)
        stats = sb("stats", [P, 2, 6], F32)
        moments = sb("moments", [P, 2, 2], F32)
        var_eps = sb("var_eps", [P, 2], F32)
        rstd = sb("rstd", [P, 2], F32)
        xnorm = sb("xnorm", [P, RING, T], F32)
        qk = sb("qk", [P, RING, 2, T], F32)
        qk_swap = sb("qk_swap", [P, RING, 2, T], F32)
        qk_rot = sb("qk_rot", [P, RING, 2, T], F32)
        rot_sin = sb("rot_sin", [P, 2, T], F32)
        values = sb("values", [P, RING, TT, G, 32], F32)
        rest = sb("rest", [P, 2, T], F32)
        parts = sb("parts", [P, RING, 2, PARTS, T], BF16)
        q_rows = sb("q_rows", [P, RING, G, T], BF16)
        k_rows = sb("k_rows", [P, RING, G, T], BF16)
        maxima = sb("maxima", [P, TT, G], F32)
        max_rest = sb("max_rest", [P, TT, HEADS], F32)
        max_parts = sb("max_parts", [P, 2, TT, PARTS, HEADS], BF16)
        max_rows = sb("max_rows", [PARTS * HEADS, 2, T], BF16)
        probs = sb("probs", [P, G, TT, T], F32)
        raw = sb("raw", [P, 2, T], F32)
        inv_sums = sb("inv_sums", [P, TT * HEADS], F32)
        by_target = sb("by_target", [P, TT, 2, C], F32)
        attended = sb("attended", [P, T], F32)
        xres = sb("xres", [P, RING, T], F32)
        x2 = sb("x2", [P, RING, T], F32)
        x2norm = sb("x2norm", [P, T], F32)
        x2hi = sb("x2hi", [P, TT, P], F16)
        x2lo = sb("x2lo", [P, TT, P], F16)
        hid = sb("hid", [P, HT * P], F32)
        hid_sq = sb("hid_sq", [P, HT * P], F32)
        hid_hi = sb("hid_hi", [P, HT * P], F16)
        hid_lo = sb("hid_lo", [P, HT * P], F16)
        xout = sb("xout", [P, RING, T], F32)

        max_ps = psum("max_ps", [P, 2, TT, T], F32)
        exp_ps = psum("exp_ps", [P, RING, TT, T], F32)
        att_ps = psum("att_ps", [P, 2 * T], F32)
        small_ps = psum("small_ps", [P, 2, 2 * T], F32)

        def small(user):
            which = [user in dict(users) for users in SMALL].index(True)
            return small_ps[:, which, 0:T], which

        s_const = sem("const_loaded")
        s_wload = sem("ffn_weights_loaded")
        s_fill = sem("constants_filled")
        s_id16 = sem("ident16_made")
        s_prep = sem("prep_step")
        s_wred = sem("weight_sums")
        s_wtot = sem("weight_totals")
        s_ready = sem("ffn_weights_ready")

        s_xin = [sem(f"x_loaded{u}") for u in range(RING)]
        s_cin = [sem(f"ctx_loaded{u}") for u in range(RING)]
        s_xres = [sem(f"xres_loaded{u}") for u in range(RING)]
        s_swap = [sem(f"swapped{u}") for u in range(RING)]
        s_wrote = [sem(f"parts_stored{u}") for u in range(RING)]
        s_seen = sem("parts_seen")
        s_rows = [sem(f"rows_loaded{u}") for u in range(RING)]
        s_mrow = [[sem(f"max_rows_loaded{b}{u}") for u in range(RING)] for b in range(2)]
        s_out = [sem(f"out_free{u}") for u in range(RING)]

        s_ln1 = sem("ln1_step")
        s_stats = sem("stats_seen")
        s_pow1 = sem("ln1_rstd")
        s_ln2 = sem("ln2_step")
        s_pow2 = sem("ln2_rstd")
        s_k = sem("k_made")
        s_v = sem("v_made")
        s_q = sem("q_made")
        s_kq = sem("kq_kept")
        s_vk = sem("v_kept")
        s_taken = [sem("small0_taken"), sem("small1_taken")]
        s_rot = sem("rotate_step")
        s_hi = sem("high_parts")
        s_rest = sem("rest_made")
        s_mid = sem("middle_parts")
        s_lo = sem("low_parts")
        s_sc = sem("max_scores_made")
        s_mx = sem("maxima_made")
        s_mc = sem("max_parts_step")
        s_mt = sem("max_turned")
        s_mk = sem("max_rows_kept")
        s_es = sem("exp_scores_made")
        s_ex = sem("probs_made")
        s_pv = sem("attended_made")
        s_raw = sem("raw_kept")
        s_at = sem("raw_turned")
        s_nm = sem("normalise_step")
        s_bk = sem("attended_turned")
        s_ak = sem("attended_kept")
        s_wo = sem("wo_made")
        s_xt = sem("x2_turned")
        s_xh = sem("x2_high")
        s_xl = sem("x2_low")
        s_hd = sem("hidden_made")
        s_hr = sem("hidden_kept")
        s_hh = sem("hidden_high")
        s_h2 = sem("hidden_squared")
        s_hl = sem("hidden_low")
        s_f2 = sem("ffn2_made")
        s_fin = sem("xout_made")

        block = ctx.enter_context(nc.Block())

        @block.sync
        def _(sp):
            def load(dst, src):
                sp.dma_start(dst, src).then_inc(s_const, 16)

            def rows(dram, n):
                first = n.times(P, 0)
                if isinstance(first, int):
                    return dram[first:first + P, :]
                return dram[bass.ds(sp.snap(first), P), :]

            def load_x(n):
                if n.real:
                    x_rows = rows(x, n)
                    if not isinstance(n.j, int) or n.c >= RING:
                        sp.wait_ge(s_ln1, n.back(RING).times(4, 4))
                    sp.dma_start(xin[:, n.slot, :], x_rows).then_inc(s_xin[n.slot], 16)

            def load_ctx(n):
                if n.real:
                    ctx_rows = rows(ctx_in, n)
                    if not isinstance(n.j, int) or n.c >= RING:
                        sp.wait_ge(s_v, n.back(RING).times(1, 1))
                    sp.dma_start(cin[:, n.slot, :], ctx_rows).then_inc(s_cin[n.slot], 16)

            for u in range(RING):
                sp.sem_inc(s_out[u], 16)
            load_x(Count(0, 0))
            load_ctx(Count(0, 0))
            for dst, src in ((wk[:], wk_bd), (bk[:], bk_col), (wv[:], wv_bd), (wq[:], wq_bd), (bq[:], bq_col),
                             (cos[:], cos_t), (sin[:], sin_t), (ident[:], ident_t),
                             (wo[:], wo_bd), (bv[:], bv_col), (bo[:], bo_col)):
                load(dst, src)
            sp.dma_start(wfc[:], wfc_t).then_inc(s_wload, 16)
            sp.dma_start(wproj[:], wproj_t).then_inc(s_wload, 16)

            def store_maxima(n, b):
                if not n.real:
                    return
                u = n.slot
                sp.wait_ge(s_mk, n.times(2, 1 + b))
                sp.dma_start(q_rows[ROWS:MROWS, u, b * HEADS:(b + 1) * HEADS, :],
                             max_rows[:, b, :]).then_inc(s_mrow[b][u], 16)

            def step(s):
                load_x(s.back(-1))
                store_maxima(s.back(3), 1)
                n = split = s.back(1)
                if n.real:
                    u = n.slot
                    sp.wait_ge(s_lo, n.times(1, 1))
                    sp.wait_ge(s_mid, n.times(1, 1))
                    sp.dma_start(spread[u].rearrange("a p r t -> r (a p) t"),
                                 parts[:, u, :, :, :].rearrange("r a p t -> r (a p) t")).then_inc(s_wrote[u], 16)
                n = s
                if n.real:
                    sp.wait_ge(s_kq, n.times(2, 2))
                    for half in range(2):
                        sp.dma_start(qk_swap[64 * half:64 * half + 64, n.slot, :, :],
                                     qk[64 - 64 * half:128 - 64 * half, n.slot, :, :]).then_inc(s_swap[n.slot], 16)
                load_ctx(s.back(-1))
                n = s.back(3)
                if n.real:
                    x_rows = rows(x, n)
                    if not isinstance(n.j, int) or n.c >= RING:
                        sp.wait_ge(s_ln2, n.back(RING).times(5, 1))
                    sp.dma_start(xres[:, n.slot, :], x_rows).then_inc(s_xres[n.slot], 16)
                n = split
                if n.real:
                    u = n.slot
                    sp.wait_ge(s_wrote[u], n.turns(16))
                    sp.sem_inc(s_seen, 1)
                    if not isinstance(n.j, int) or n.c >= RING:
                        sp.wait_ge(s_es, n.back(RING).times(G, G))
                    else:
                        sp.wait_ge(s_fill, 3 + u)
                    for r in range(PARTS):
                        sp.dma_start(
                            q_rows[r * 24:r * 24 + 24, u, :, :],
                            spread[u, 0, r].rearrange("(c g) t -> c (g t)", g=G).unsqueeze(0)
                            .broadcast_to([PARTS, KC, G * T])).then_inc(s_rows[u], 16)
                    sp.dma_start(
                        k_rows[0:ROWS, u, :, :],
                        spread[u, 1].rearrange("p (c g) t -> (p c) (g t)", g=G).unsqueeze(0)
                        .broadcast_to([PARTS, PARTS * KC, G * T])).then_inc(s_rows[u], 16)
                n = s.back(6)
                if n.real:
                    out_rows = rows(out, n)
                    sp.wait_ge(s_fin, n.times(1, 1))
                    sp.dma_start(out_rows, xout[:, n.slot, :]).then_inc(s_out[n.slot], 16)
                store_maxima(s.back(2), 0)

            run_steps(sp, step)
            for u in range(RING):
                sp.wait_ge(s_out[u], 16 + 16 * len(range(u, PAIRS, RING)))

        @block.gpsimd
        def _(pool):
            pool.memset(ones[:], 1.0).then_inc(s_fill, 1)
            pool.memset(minus_half[:], -0.5).then_inc(s_fill, 1)
            pool.wait_ge(s_fill, 2)
            for u in range(RING):
                pool.memset(k_rows[64:96, u, :, :], 1.0).then_inc(s_fill, 1)
            pool.wait_ge(s_fill, 5)
            pool.memset(values[:], 0.0).then_inc(s_fill, 1)
            pool.wait_ge(s_fill, 6)
            for u in range(RING):
                by_head = values[:, u, :, :, :].rearrange("p t (j o) c -> p (t j) o c", o=2)
                pool.memset(by_head[:, :, 0, 16:24], 1.0).then_inc(s_fill, 1)
                pool.memset(by_head[:, :, 1, 24:32], 1.0).then_inc(s_fill, 1)

            def rstd_of(n, at, done, k, more, made):
                if n.real:
                    pool.wait_ge(done, n.times(k, more))
                    pool.tensor_tensor(rstd[:, at:at + 1], var_eps[:, at:at + 1], minus_half[:], ALU.pow)\
                        .then_inc(made, 1)

            def step(s):
                n = s.back(1)
                if n.real:
                    u = n.slot
                    pool.wait_ge(s_hi, n.times(1, 1))
                    pool.tensor_tensor(rest[:], qk_rot[:, u, :, :], parts[:, u, :, 0, :], ALU.subtract)\
                        .then_inc(s_rest, 1)
                    pool.wait_ge(s_rest, n.times(1, 1))
                    pool.wait_ge(s_mid, n.times(1, 1))
                    pool.tensor_tensor(parts[:, u, :, 2, :], rest[:], parts[:, u, :, 1, :], ALU.subtract)\
                        .then_inc(s_lo, 1)
                n = s
                if n.real:
                    u = n.slot
                    cos2 = cos[:].unsqueeze(1).broadcast_to([P, 2, T])
                    sin2 = sin[:].unsqueeze(1).broadcast_to([P, 2, T])
                    if isinstance(s.j, int) and s.c == 0:
                        pool.wait_ge(s_const, 16 * 11)
                    pool.wait_ge(s_kq, n.times(2, 2))
                    pool.tensor_tensor(qk_rot[:, u, :, :], qk[:, u, :, :], cos2, ALU.mult).then_inc(s_rot, 1)
                rstd_of(s.back(-1), 0, s_ln1, 4, 3, s_pow1)
                if n.real:
                    pool.wait_ge(s_swap[u], n.turns(32))
                    pool.tensor_tensor(rot_sin[:], qk_swap[:, u, :, :], sin2, ALU.mult).then_inc(s_rot, 1)
                    pool.wait_ge(s_rot, n.times(3, 2))
                    pool.tensor_tensor(qk_rot[:, u, :, :], qk_rot[:, u, :, :], rot_sin[:], ALU.add)\
                        .then_inc(s_rot, 1)
                n = s.back(5)
                if n.real:
                    pool.wait_ge(s_hr, n.times(3, 3))
                    pool.tensor_tensor(hid_sq[:], hid[:], hid[:], ALU.mult).then_inc(s_h2, 1)
                    pool.wait_ge(s_h2, n.times(1, 1))
                    pool.wait_ge(s_hh, n.times(1, 1))
                    if not isinstance(n.j, int) or n.c >= 1:
                        pool.wait_ge(s_f2, n.times(1, 0))
                    pool.tensor_tensor(hid_lo[:], hid_sq[:], hid_hi[:], ALU.subtract).then_inc(s_hl, 1)
                rstd_of(s.back(4), 1, s_ln2, 5, 4, s_pow2)

            rstd_of(Count(0, 0), 0, s_ln1, 4, 3, s_pow1)
            run_steps(pool, step)

        @block.scalar
        def _(act):
            act.wait_ge(s_const, 16 * 11)
            act.activation(ident16[:], ident[:], ACT.Copy).then_inc(s_id16, 1)

            def keep_kq(n, which, made, user):
                if n.real:
                    src, which_bank = small(user)
                    act.wait_ge(made, n.times(1, 1))
                    if which == 1 and (not isinstance(n.j, int) or n.c >= RING):
                        act.wait_ge(s_rot, n.back(RING).times(3, 3))
                    act.activation(qk[:, n.slot, which, :], src, ACT.Identity,
                                   bias=(bk if which else bq)[:, 0:1]).then_inc(s_kq, 1)
                    act.wait_ge(s_kq, n.times(2, 1 if which else 2))
                    act.sem_inc(s_taken[which_bank], 1)

            def keep_v(n):
                if n.real:
                    src, which_bank = small("v")
                    act.wait_ge(s_v, n.times(1, 1))
                    if not isinstance(n.j, int) or n.c >= RING:
                        act.wait_ge(s_pv, n.back(RING).times(8, 8))
                    else:
                        act.wait_ge(s_fill, 12)
                    dst = values[:, n.slot, :, :, :].rearrange("p t g c -> p (t g c)")
                    for o in range(2):
                        act.activation(
                            dst.rearrange("p (m o c) -> p m o c", o=2, c=32)[:, :, o, 8 * o:8 * o + 8],
                            src.rearrange("p (m o c) -> p m o c", o=2, c=8)[:, :, o, :], ACT.Copy)\
                            .then_inc(s_vk, 1)
                    act.wait_ge(s_vk, n.times(2, 2))
                    act.sem_inc(s_taken[which_bank], 1)

            def keep_max(n, b):
                if n.real:
                    src, which_bank = small(f"max{b}")
                    act.wait_ge(s_mt, n.times(2, 1 + b))
                    if not isinstance(n.j, int) or n.c >= 1:
                        act.wait_ge(s_mrow[b][n.back(1).slot], n.back(1).turns(16))
                    turned = src[:, 0:P].bitcast(BF16)
                    act.activation(max_rows[:, b, :], turned[0:PARTS * HEADS, :], ACT.Copy).then_inc(s_mk, 1)
                    act.wait_ge(s_mk, n.times(2, 1 + b))
                    act.sem_inc(s_taken[which_bank], 1)

            def keep_raw(n, b):
                if n.real:
                    act.wait_ge(s_pv, n.times(8, 4 * b + 4))
                    if not isinstance(n.j, int) or n.c >= 1:
                        act.wait_ge(s_at, n.times(2, b - 1))
                    act.activation(raw[:, b, :], att_ps[:, 0:T], ACT.Copy).then_inc(s_raw, 1)

            def keep_attended(n):
                if n.real:
                    src, which_bank = small("back")
                    act.wait_ge(s_bk, n.times(1, 1))
                    if not isinstance(n.j, int) or n.c >= 1:
                        act.wait_ge(s_wo, n.times(1, 0))
                    act.activation(attended[:], src, ACT.Copy).then_inc(s_ak, 1)
                    act.wait_ge(s_ak, n.times(1, 1))
                    act.sem_inc(s_taken[which_bank], 1)

            def exp(n, k):
                if n.real:
                    act.wait_ge(s_es, n.times(G, k + 1))
                    if not isinstance(n.j, int) or n.c >= 1:
                        act.wait_ge(s_pv, n.times(8, -8 + 2 * (k // 4) + 2))
                    act.activation(probs[:, k, :, :], exp_ps[:, (n.slot + k) % RING, :, :], ACT.Exp, scale=SCALE)\
                        .then_inc(s_ex, 1)

            def high(n):
                if n.real:
                    act.wait_ge(s_rot, n.times(3, 3))
                    if not isinstance(n.j, int) or n.c >= RING:
                        act.wait_ge(s_wrote[n.slot], n.turns(16, -16))
                    act.activation(parts[:, n.slot, :, 0, :], qk_rot[:, n.slot, :, :], ACT.Copy).then_inc(s_hi, 1)

            def middle(n):
                if n.real:
                    act.wait_ge(s_rest, n.times(1, 1))
                    act.activation(parts[:, n.slot, :, 1, :], rest[:], ACT.Copy).then_inc(s_mid, 1)

            def relu(n, i):
                if n.real:
                    src, which_bank = small(f"hid{i}")
                    act.wait_ge(s_hd, n.times(3, i + 1))
                    if i == 0 and (not isinstance(n.j, int) or n.c >= 1):
                        act.wait_ge(s_h2, n.times(1, 0))
                        act.wait_ge(s_hh, n.times(1, 0))
                    cols = T if i < 2 else P
                    act.activation(hid[:, i * T:i * T + cols], src[:, 0:cols], ACT.Relu,
                                   scale=RELU_SCALE).then_inc(s_hr, 1)
                    act.wait_ge(s_hr, n.times(3, i + 1))
                    act.sem_inc(s_taken[which_bank], 1)

            def square(n):
                if n.real:
                    act.wait_ge(s_hr, n.times(3, 3))
                    if not isinstance(n.j, int) or n.c >= 1:
                        act.wait_ge(s_f2, n.times(1, 0))
                        act.wait_ge(s_hl, n.times(1, 0))
                    act.activation(hid_hi[:], hid[:], ACT.Square).then_inc(s_hh, 1)

            def x2_high(n):
                if n.real:
                    src, _ = small("xT")
                    act.wait_ge(s_xt, n.times(1, 1))
                    if not isinstance(n.j, int) or n.c >= 1:
                        act.wait_ge(s_hd, n.times(3, 0))
                    act.activation(x2hi[:].rearrange("p a b -> p (a b)"), src, ACT.Copy).then_inc(s_xh, 1)

            def step(s):
                maxima_of, attending, ending = s.back(2), s.back(3), s.back(4)
                high(s.back(1))
                for k in range(G):
                    exp(attending, k)
                    if k == 1:
                        middle(s.back(1))
                    if k == 2:
                        keep_max(attending, 1)
                        keep_kq(s, 1, s_k, "k")
                    if k == 3:
                        x2_high(s.back(5))
                    if k == 4:
                        keep_kq(s, 0, s_q, "q")
                    if k == 5:
                        keep_raw(ending, 1)
                        keep_v(maxima_of)
                    if k == 6:
                        relu(s.back(5), 0)
                    if k == 8:
                        relu(s.back(5), 1)
                    if k == 10:
                        relu(s.back(5), 2)
                        keep_attended(ending)
                        square(s.back(5))
                    if k == 11:
                        keep_raw(attending, 0)
                    if k == 12:
                        keep_max(maxima_of, 0)

            run_steps(act, step)

        @block.vector
        def _(dve):
            def stats_of(src, at, done):
                dve.bn_stats(stats[:, at, :], src).then_inc(done, 1)

            def moments_of(n, at, done, k, first):
                dve.wait_ge(done, n.times(k, first + 1))
                dve.sem_inc(s_stats, 1)
                dve.bn_aggr(moments[:, at, :], stats[:, at, :]).then_inc(done, 1)

            def var_eps_of(n, at, done, k, first):
                dve.wait_ge(done, n.times(k, first + 2))
                dve.tensor_scalar(var_eps[:, at:at + 1], moments[:, at, 1:2], EPS, None, ALU.add)\
                    .then_inc(done, 1)

            def normalised(n, src, at, dst, done, made):
                dve.wait_ge(made, n.times(1, 1))
                dve.tensor_scalar(dst, src, moments[:, at, 0:1], rstd[:, at:at + 1], ALU.subtract, ALU.mult)\
                    .then_inc(done, 1)

            def ln1(n, i):
                if n.real:
                    if i == 0:
                        dve.wait_ge(s_xin[n.slot], n.turns(16))
                        stats_of(xin[:, n.slot, :], 0, s_ln1)
                    if i == 1:
                        moments_of(n, 0, s_ln1, 4, 0)
                    if i == 2:
                        var_eps_of(n, 0, s_ln1, 4, 0)
                    if i == 3:
                        if not isinstance(n.j, int) or n.c >= RING:
                            dve.wait_ge(s_q, n.back(RING).times(1, 1))
                        normalised(n, xin[:, n.slot, :], 0, xnorm[:, n.slot, :], s_ln1, s_pow1)

            def ln2(n, i):
                if n.real:
                    u = n.slot
                    if i == 0:
                        src, which_bank = small("wo")
                        dve.wait_ge(s_wo, n.times(1, 1))
                        dve.wait_ge(s_xres[u], n.turns(16))
                        dve.scalar_tensor_tensor(out=x2[:, u, :], in0=src, scalar=out_bias[:, 0:1],
                                                 in1=xres[:, u, :], op0=ALU.add, op1=ALU.add).then_inc(s_ln2, 1)
                    if i == 1:
                        dve.wait_ge(s_ln2, n.times(5, 1))
                        dve.sem_inc(s_taken[small("wo")[1]], 1)
                        stats_of(x2[:, u, :], 1, s_ln2)
                    if i == 2:
                        moments_of(n, 1, s_ln2, 5, 1)
                    if i == 3:
                        var_eps_of(n, 1, s_ln2, 5, 1)
                    if i == 4:
                        if not isinstance(n.j, int) or n.c >= 1:
                            dve.wait_ge(s_xt, n.times(1, 0))
                        normalised(n, x2[:, u, :], 1, x2norm[:], s_ln2, s_pow2)

            def x2_low(n):
                if n.real:
                    src, which_bank = small("xT")
                    dve.wait_ge(s_xh, n.times(1, 1))
                    if not isinstance(n.j, int) or n.c >= 1:
                        dve.wait_ge(s_hd, n.times(3, 0))
                    dve.tensor_tensor(x2lo[:].rearrange("p a b -> p (a b)"), src,
                                      x2hi[:].rearrange("p a b -> p (a b)"), ALU.subtract).then_inc(s_xl, 1)
                    dve.wait_ge(s_xl, n.times(1, 1))
                    dve.sem_inc(s_taken[which_bank], 1)

            def head_max(n, k):
                if n.real:
                    g = k // HEADS * HEADS + ORDER[k % HEADS]
                    dve.wait_ge(s_sc, n.times(G, k + 1))
                    dve.tensor_reduce(maxima[:, :, g], max_ps[:, k % 2, :, :], AX_X, ALU.max).then_inc(s_mx, 1)

            def split_max(n, b, i):
                if n.real:
                    m = maxima[:, :, b * HEADS:(b + 1) * HEADS]
                    part = [max_parts[:, b, :, p, :] for p in range(PARTS)]
                    if i:
                        dve.wait_ge(s_mc, n.times(8, 4 * b + i))
                    if i == 0:
                        dve.wait_ge(s_mx, n.times(G, (b + 1) * HEADS))
                        if not isinstance(n.j, int) or n.c >= 1:
                            dve.wait_ge(s_mt, n.times(2, b - 1))
                        dve.tensor_scalar(part[0], m, -1.0, None, ALU.mult).then_inc(s_mc, 1)
                    if i == 1:
                        dve.scalar_tensor_tensor(out=max_rest[:], in0=m, scalar=-1.0, in1=part[0], op0=ALU.mult,
                                                 op1=ALU.subtract).then_inc(s_mc, 1)
                    if i == 2:
                        dve.tensor_copy(part[1], max_rest[:]).then_inc(s_mc, 1)
                    if i == 3:
                        dve.tensor_tensor(part[2], max_rest[:], part[1], ALU.subtract).then_inc(s_mc, 1)

            def invert(n, b):
                if n.real:
                    heads = small(f"att{b}")[0].rearrange("p (m o c) -> p m o c", o=4, c=KC)
                    dve.wait_ge(s_at, n.times(2, b + 1))
                    dve.reciprocal(inv_sums[:].rearrange("p (m o) -> p m o", o=2), heads[:, :, 2:4, 0])\
                        .then_inc(s_nm, 1)

            def divide(n, b):
                if n.real:
                    src, which_bank = small(f"att{b}")
                    heads = src.rearrange("p (m o c) -> p m o c", o=4, c=KC)
                    dve.wait_ge(s_nm, n.times(6, 3 * b + 1))
                    if not isinstance(n.j, int) or n.c >= 1:
                        dve.wait_ge(s_bk, n.times(1, 0))
                    half_heads = HEADS // 2
                    for t in range(TT):
                        at = slice(t * half_heads, (t + 1) * half_heads)
                        dve.tensor_tensor(
                            by_target[:, t, b, :].rearrange("p (j o c) -> p j o c", o=2, c=KC),
                            heads[:, at, 0:2, :],
                            inv_sums[:].rearrange("p (m o) -> p m o", o=2)[:, at, :].unsqueeze(3)
                            .broadcast_to([P, half_heads, 2, KC]), ALU.mult).then_inc(s_nm, 1)
                    dve.wait_ge(s_nm, n.times(6, 3 * b + 3))
                    dve.sem_inc(s_taken[which_bank], 1)

            def finish(n):
                if n.real:
                    u = n.slot
                    src, which_bank = small("ffn2")
                    dve.wait_ge(s_f2, n.times(1, 1))
                    dve.wait_ge(s_out[u], n.turns(16))
                    dve.scalar_tensor_tensor(out=xout[:, u, :], in0=src, scalar=fscale[:, 1:2], in1=x2[:, u, :],
                                             op0=ALU.mult, op1=ALU.add).then_inc(s_fin, 1)
                    dve.wait_ge(s_fin, n.times(1, 1))
                    dve.sem_inc(s_taken[which_bank], 1)

            def prepare_sums():
                dve.wait_ge(s_wload, 32)
                dve.tensor_reduce(wsum[:, 0:1], wfc[:].rearrange("p a b -> p (a b)"), AX_X, ALU.add,
                                  apply_absolute_value=True).then_inc(s_wred, 1)
                dve.tensor_reduce(wsum[:, 1:2], wproj[:].rearrange("p a b -> p (a b)"), AX_X, ALU.add,
                                  apply_absolute_value=True).then_inc(s_wred, 1)

            def prepare_weights():
                dve.wait_ge(s_wtot, 1)
                dve.wait_ge(s_const, 16 * 11)
                dve.tensor_scalar(out_bias[:], att_ps[:, 4:5], bo[:, 0:1], None, ALU.add).then_inc(s_prep, 1)
                dve.tensor_scalar(wmean[:], att_ps[:, 0:2], 1.0 / (HID * T), 1e-5, ALU.mult, ALU.max)\
                    .then_inc(s_prep, 1)
                dve.wait_ge(s_prep, 2)
                dve.tensor_scalar(wthr[:], wmean[:], 0.7, None, ALU.mult).then_inc(s_prep, 1)
                dve.tensor_scalar(wnthr[:], wmean[:], -0.7, None, ALU.mult).then_inc(s_prep, 1)
                dve.tensor_tensor(fscale[:, 0:1], wmean[:, 0:1], wmean[:, 0:1], ALU.mult).then_inc(s_prep, 1)
                dve.wait_ge(s_prep, 5)
                dve.tensor_scalar(fscale[:, 1:2], fscale[:, 0:1], wmean[:, 1:2], RELU_SCALE ** -2,
                                  ALU.mult, ALU.mult).then_inc(s_prep, 1)
                for i, (w, w3) in enumerate(((wfc, fc3), (wproj, proj3))):
                    flat, flat3 = (t[:].rearrange("p a b -> p (a b)") for t in (w, w3))
                    dve.tensor_scalar(below[:], flat, wnthr[:, i:i + 1], None, ALU.is_lt).then_inc(s_prep, 1)
                    dve.wait_ge(s_prep, 7 + 2 * i)
                    dve.scalar_tensor_tensor(out=flat3, in0=flat, scalar=wthr[:, i:i + 1], in1=below[:],
                                             op0=ALU.is_gt, op1=ALU.subtract).then_inc(s_prep, 1)
                    dve.wait_ge(s_prep, 8 + 2 * i)
                dve.sem_inc(s_ready, 1)

            def step(s):
                maxima_of, attending, ending = s.back(2), s.back(3), s.back(4)
                if isinstance(s.j, int) and s.c == 0:
                    prepare_sums()
                    prepare_weights()
                split_max(attending, 1, 0)
                ln2(s.back(5), 4)
                split_max(attending, 1, 1)
                for k in range(G):
                    head_max(maxima_of, k)
                    if k == 0:
                        split_max(attending, 1, 2)
                        finish(s.back(6))
                        split_max(attending, 1, 3)
                    if k == 4:
                        x2_low(s.back(5))
                    if k in (1, 2, 3):
                        ln1(s.back(-1), k - 1)
                    if k == 7:
                        invert(ending, 1)
                    if k == 8:
                        divide(ending, 1)
                        split_max(maxima_of, 0, 0)
                    if k == 9:
                        split_max(maxima_of, 0, 1)
                    if k == 10:
                        split_max(maxima_of, 0, 2)
                    if k == 11:
                        split_max(maxima_of, 0, 3)
                    if k in (12, 13, 14, 15):
                        ln2(ending, k - 12)
                    if k == 9:
                        ln1(s.back(-1), 3)
                    if k == 14:
                        invert(attending, 0)
                divide(attending, 0)

            for i in range(4):
                ln1(Count(0, 0), i)
            run_steps(dve, step)

        @block.tensor
        def _(pe):
            def claim(user, s):
                dst, which = small(user)
                before = small_before(which, user, s)
                if not isinstance(before, int) or before > 0:
                    pe.wait_ge(s_taken[which], before)
                return dst

            def make_k(s):
                if s.real:
                    dst = claim("k", s)
                    pe.wait_ge(s_cin[s.slot], s.turns(16))
                    pe.matmul(dst, wk[:], cin[:, s.slot, :], start=True, stop=True).then_inc(s_k, 1)

            def make_v(n, s):
                if n.real:
                    dst = claim("v", s)
                    for t in range(TT):
                        mm = pe.matmul(dst[:, t * P:(t + 1) * P], cin[:, n.slot, t * P:(t + 1) * P], wv[:],
                                       start=True, stop=True)
                    mm.then_inc(s_v, 1)

            def make_q(s):
                if s.real:
                    dst = claim("q", s)
                    pe.wait_ge(s_ln1, s.times(4, 4))
                    pe.matmul(dst, wq[:], xnorm[:, s.slot, :], start=True, stop=True).then_inc(s_q, 1)

            def turn_max(n, b, s):
                if n.real:
                    turned = claim(f"max{b}", s)[:, 0:P].bitcast(BF16)
                    if isinstance(n.j, int) and n.c == 0:
                        pe.wait_ge(s_id16, 1)
                    pe.wait_ge(s_mc, n.times(8, 4 * b + 4))
                    for t in range(TT):
                        mm = pe.transpose(turned[0:PARTS * HEADS, t * P:(t + 1) * P],
                                          max_parts[:, b, t, :, :].rearrange("p a h -> p (a h)"), ident16[:])
                    mm.then_inc(s_mt, 1)

            def max_scores(n, k):
                if n.real:
                    u, g = n.slot, k // HEADS * HEADS + ORDER[k % HEADS]
                    if k == 0:
                        pe.wait_ge(s_rows[u], n.turns(64))
                    if k >= 2 or not isinstance(n.j, int) or n.c >= 1:
                        pe.wait_ge(s_mx, n.times(G, k - 1))
                    for t in range(TT):
                        mm = pe.matmul(max_ps[:, k % 2, t, :], q_rows[0:ROWS, u, g, t * P:(t + 1) * P],
                                       k_rows[0:ROWS, u, g, :], start=True, stop=True)
                    mm.then_inc(s_sc, 1)

            def exp_scores(n, k):
                if n.real:
                    u, g = n.slot, k // HEADS * HEADS + ORDER[k % HEADS]
                    if k % HEADS == 0:
                        pe.wait_ge(s_mrow[k // HEADS][u], n.turns(16))
                    if k >= RING or not isinstance(n.j, int) or n.c >= 1:
                        pe.wait_ge(s_ex, n.times(G, k + 1 - RING))
                    for t in range(TT):
                        mm = pe.matmul(exp_ps[:, (u + k) % RING, t, :], k_rows[0:MROWS, u, g, t * P:(t + 1) * P],
                                       q_rows[0:MROWS, u, g, :], start=True, stop=True)
                    mm.then_inc(s_es, 1)

            def attend(n, part):
                if n.real:
                    quad, t = part // 2, part % 2
                    b, odd = quad // 2, quad % 2
                    if t == 0:
                        pe.wait_ge(s_ex, n.times(G, 4 * quad + 4))
                    if part == 0:
                        pe.wait_ge(s_vk, n.times(2, 2))
                        if isinstance(n.j, int) and n.c == 0:
                            pe.wait_ge(s_ready, 1)
                    if part == 4 or part == 0 and (not isinstance(n.j, int) or n.c >= 1):
                        pe.wait_ge(s_raw, n.times(2, b))
                    for j in range(4):
                        mm = pe.matmul(att_ps[32 * j:32 * j + 32, 0:T],
                                       values[:, n.slot, t, b * HEADS + 2 * j + odd, :],
                                       probs[:, 4 * quad + j, t, :],
                                       start=(part % 4 == 0), stop=(part % 4 == 3))
                    mm.then_inc(s_pv, 1)

            def turn(dst, parts_in, done):
                for t in range(TT):
                    mm = pe.transpose(dst[:, t * P:(t + 1) * P], parts_in[t], ident[:])
                mm.then_inc(done, 1)

            def turn_raw(n, b, s):
                if n.real:
                    dst = claim(f"att{b}", s)
                    pe.wait_ge(s_raw, n.times(2, b + 1))
                    turn(dst, [raw[:, b, t * P:(t + 1) * P] for t in range(TT)], s_at)

            def turn_back(n, s):
                if n.real:
                    dst = claim("back", s)
                    pe.wait_ge(s_nm, n.times(6, 6))
                    turn(dst, [by_target[:, t, :, :].rearrange("p b c -> p (b c)") for t in range(TT)], s_bk)

            def project_out(n, s):
                if n.real:
                    dst = claim("wo", s)
                    pe.wait_ge(s_ak, n.times(1, 1))
                    pe.matmul(dst, wo[:], attended[:], start=True, stop=True).then_inc(s_wo, 1)

            def turn_x2(n, s):
                if n.real:
                    dst = claim("xT", s)
                    pe.wait_ge(s_ln2, n.times(5, 5))
                    turn(dst, [x2norm[:, t * P:(t + 1) * P] for t in range(TT)], s_xt)

            def hidden(n, i, s):
                if n.real:
                    dst = claim(f"hid{i}", s)
                    if i == 0:
                        pe.wait_ge(s_xl, n.times(1, 1))
                    for h in range(2 * i, min(2 * i + 2, HT)):
                        at = (h - 2 * i) * P
                        for m, (t, half) in enumerate((t, half) for half in (x2hi, x2lo) for t in range(TT)):
                            mm = pe.matmul(dst[:, at:at + P], fc3[:, t, h * P:(h + 1) * P],
                                           half[:, t, :], start=(m == 0), stop=(m == 3))
                    mm.then_inc(s_hd, 1)

            def ffn2(n, s):
                if n.real:
                    dst = claim("ffn2", s)
                    pe.wait_ge(s_hl, n.times(1, 1))
                    for m, (h, half) in enumerate((h, half) for half in (hid_hi, hid_lo) for h in range(HT)):
                        mm = pe.matmul(dst, half[:, h * P:(h + 1) * P], proj3[:, h, :],
                                       start=(m == 0), stop=(m == 2 * HT - 1))
                    mm.then_inc(s_f2, 1)

            pe.wait_ge(s_const, 16 * 11)
            pe.wait_ge(s_fill, 1)

            def totals():
                pe.wait_ge(s_wred, 2)
                pe.matmul(att_ps[:, 0:2], ones[:], wsum[:], start=True, stop=True)
                pe.matmul(att_ps[:, 4:5], wo[:], bv[:], start=True, stop=True).then_inc(s_wtot, 1)

            def step(s):
                maxima_of, attending, ending, feeding = s.back(2), s.back(3), s.back(4), s.back(5)
                for k in range(G):
                    if k in (0, 2, 4):
                        attend(ending, 5 + k // 2)
                    if k in (7, 8, 10, 11, 14):
                        attend(attending, (7, 8, 10, 11, 14).index(k))
                    exp_scores(attending, k)
                    max_scores(maxima_of, k)
                    if k == 2:
                        turn_max(attending, 1, s)
                        make_k(s)
                    if k == 3:
                        turn_x2(feeding, s)
                    if k == 4:
                        make_q(s)
                        if isinstance(s.j, int) and s.c == 0:
                            totals()
                    if k == 5:
                        make_v(maxima_of, s)
                    if k == 6:
                        hidden(feeding, 0, s)
                    if k == 7:
                        turn_raw(ending, 1, s)
                    if k == 8:
                        hidden(feeding, 1, s)
                    if k == 9:
                        hidden(feeding, 2, s)
                    if k == 10:
                        turn_back(ending, s)
                    if k == 12:
                        project_out(ending, s)
                        turn_max(maxima_of, 0, s)
                    if k == 14:
                        turn_raw(attending, 0, s)
                    if k == 15:
                        ffn2(feeding, s)

            run_steps(pe, step)


def kernel(x, ctx_2048, L0_xattn_Wq, L0_xattn_bq, L0_xattn_Wk, L0_xattn_bk, L0_xattn_Wv, L0_xattn_bv,
           L0_xattn_Wo, L0_xattn_bo, L0_ffn_w_fc, L0_ffn_w_proj):
    import numpy as np
    import concourse.bacc as bacc
    from concourse.bass_utils import run_bass_kernel_spmd

    def by_channel(w):
        t = np.zeros((2, C, KC, 2, HEADS), np.float32)
        for b in range(2):
            t[b, :, :, b, :] = np.asarray(w).reshape(HEADS, KC, C).transpose(2, 1, 0)
        return t.reshape(P, P)

    def bias_by_channel(v):
        t = np.zeros((KC, 2, HEADS), np.float32)
        for b in range(2):
            t[:, b, :] = np.asarray(v).reshape(HEADS, KC).transpose(1, 0)
        return t.reshape(P, 1)

    wv_bd = np.zeros((2, C, 2, C), np.float32)
    wo_bd = np.zeros((2, C, 2, C), np.float32)
    bo_col = np.zeros((2, C), np.float32)
    bv_col = np.zeros((2, C), np.float32)
    for b in range(2):
        wv_bd[b, :, b, :] = np.asarray(L0_xattn_Wv).T
        wo_bd[b, :, b, :] = np.asarray(L0_xattn_Wo).T
        bo_col[b] = np.asarray(L0_xattn_bo)
        bv_col[b] = np.asarray(L0_xattn_bv)

    inv = (1.0 / np.float32(10000.0) ** (np.arange(0, KC, 2, dtype=np.float32) / np.float32(KC))).astype(np.float32)
    angle = (np.arange(T, dtype=np.float32)[None, :] * np.tile(inv, 2)[:, None]).astype(np.float32)
    sign = np.repeat(np.array([-1.0, 1.0], np.float32), KC // 2)[:, None]
    cos_t = np.repeat(np.cos(angle), G, axis=0).astype(np.float32)
    sin_t = np.repeat(np.sin(angle) * sign, G, axis=0).astype(np.float32)

    arrays = {
        "x": np.asarray(x).reshape(BATCHES * C, T),
        "ctx_in": np.asarray(ctx_2048).reshape(BATCHES * C, T),
        "wq_bd": by_channel(L0_xattn_Wq), "wk_bd": by_channel(L0_xattn_Wk), "wv_bd": wv_bd.reshape(P, P),
        "wo_bd": wo_bd.reshape(P, P),
        "bq_col": bias_by_channel(L0_xattn_bq), "bk_col": bias_by_channel(L0_xattn_bk),
        "bv_col": bv_col.reshape(P, 1), "bo_col": bo_col.reshape(P, 1),
        "wfc_t": np.ascontiguousarray(np.asarray(L0_ffn_w_fc).T.reshape(TT, P, HID).transpose(1, 0, 2)),
        "wproj_t": np.ascontiguousarray(np.asarray(L0_ffn_w_proj).T.reshape(HT, P, T).transpose(1, 0, 2)),
        "cos_t": cos_t, "sin_t": sin_t, "ident_t": np.eye(P, dtype=np.float32),
    }
    nc = bacc.Bacc("TRN2", target_bir_lowering=False, num_devices=1)
    args = [nc.dram_tensor(f"in_{name}", a.shape, F32, kind="ExternalInput").ap() for name, a in arrays.items()]
    out = nc.dram_tensor("out_x", (BATCHES * C, T), F32, kind="ExternalOutput").ap()
    xattn_ffn(nc, *args, out)
    r = run_bass_kernel_spmd(nc, [{f"in_{name}": a for name, a in arrays.items()}], core_ids=[0])
    return r.results[0]["out_x"].reshape(BATCHES, C, T)
```

```python
from contextlib import ExitStack

import concourse.bass as bass
from concourse import mybir

F32 = mybir.dt.float32
BF16 = mybir.dt.bfloat16
F16 = mybir.dt.float16
ALU = mybir.AluOpType
ACT = mybir.ActivationFunctionType
AX_X = mybir.AxisListType.X

BATCHES, C, T = 32, 64, 256
HEADS = 8
KC = C // HEADS
HID = 640
PAIRS = BATCHES // 2
P = 128
G = 2 * HEADS
TT = T // P
HT = HID // P
PARTS = 3
ROWS = PARTS * PARTS * KC
MROWS = ROWS + PARTS
RING = 3
CLOCK_WARM = 3
CLOCK_HOLD = 2
EPS = 1e-5
RELU_SCALE = 1.0 / 16.0
SCALE = float(KC) ** -0.5

ORDER = [0, 2, 4, 6, 1, 3, 5, 7]

SMALL = [
    [("v", 2), ("max1", 3), ("xT", 5), ("att1", 4), ("back", 4), ("wo", 4), ("att0", 3)],
    [("k", 0), ("q", 0), ("hid0", 5), ("hid1", 5), ("hid2", 5), ("max0", 2), ("ffn2", 5)],
]
FIRST_FULL, LOOP_STEPS = 6, 9
STEPS = PAIRS + 6


class Count:

    def __init__(self, j, c):
        self.j, self.c = j, c

    def back(self, d):
        return Count(self.j, self.c - d)

    @property
    def real(self):
        return not isinstance(self.j, int) or 0 <= self.c < PAIRS

    @property
    def slot(self):
        return self.c % RING

    def times(self, k, more):
        fixed = self.c * k + more
        return fixed if isinstance(self.j, int) else self.j * (RING * k) + fixed

    def turns(self, k, more=0):
        fixed = (self.c // RING + 1) * k + more
        return fixed if isinstance(self.j, int) else self.j * k + fixed


def is_first(n):
    return isinstance(n.j, int) and n.c == 0


def no_heads_after(n):
    return isinstance(n.j, int) and n.c >= PAIRS - 2


def is_last(n):
    return isinstance(n.j, int) and n.c == PAIRS - 1


def user_before(user, s):
    users = next(users for users in SMALL if user in dict(users))
    at = [u for u, _ in users].index(user)
    line = [(u, s.back(lag)) for u, lag in users[:at]]
    for d in range(1, STEPS):
        line = [(u, s.back(d + lag)) for u, lag in users] + line
    return next(((u, n) for u, n in reversed(line)
                 if n.real and not (u.startswith("hid") and no_heads_after(n))), None)


def run_steps(engine, step):
    for c in range(FIRST_FULL):
        step(Count(0, c))
    with engine.Fori(0, LOOP_STEPS // RING, 1) as j:
        for u in range(RING):
            step(Count(j, FIRST_FULL + u))
    for c in range(FIRST_FULL + LOOP_STEPS, STEPS):
        step(Count(0, c))


def xattn_ffn(nc, x, ctx_in, wq_bd, wk_bd, wv_bd, wo_bd, bq_col, bk_col, bv_col, bo_col, wfc_t, wproj_t,
              cos_t, sin_t, ident_t, out):
    with ExitStack() as ctx:
        def sb(name, shape, dt):
            return ctx.enter_context(nc.sbuf_tensor(name, shape, dt))

        def psum(name, shape, dt):
            return ctx.enter_context(nc.psum_tensor(name, shape, dt))

        def sem(name):
            return ctx.enter_context(nc.semaphore(name))

        spread = nc.dram_tensor("spread", [RING, 2, PARTS, P, T], BF16, kind="Internal").ap()

        wq = sb("wq", [P, P], F32)
        wk = sb("wk", [P, P], F32)
        wv = sb("wv", [P, P], F32)
        wo = sb("wo", [P, P], F32)
        bq = sb("bq", [P, 1], F32)
        bk = sb("bk", [P, 1], F32)
        bv = sb("bv", [P, 1], F32)
        bo = sb("bo", [P, 1], F32)
        out_bias = sb("out_bias", [P, 1], F32)
        cos = sb("cos", [P, T], F32)
        sin = sb("sin", [P, T], F32)
        ident = sb("ident", [P, P], F32)
        ident16 = sb("ident16", [P, P], BF16)
        ones = sb("ones", [P, P], F32)
        ones16 = sb("ones16", [P, T], BF16)
        minus_half = sb("minus_half", [P, 1], F32)
        wfc = sb("wfc", [P, TT, HID], F32)
        wproj = sb("wproj", [P, HT, T], F32)
        below = sb("below", [P, 1280], F16)
        fc3 = sb("fc3", [P, TT, HID], F16)
        proj3 = sb("proj3", [P, HT, T], F16)
        wsum = sb("wsum", [P, 2], F32)
        wmean = sb("wmean", [P, 2], F32)
        wthr = sb("wthr", [P, 2], F32)
        wnthr = sb("wnthr", [P, 2], F32)
        fscale = sb("fscale", [P, 2], F32)

        xin = sb("xin", [P, RING, T], F32)
        cin = sb("cin", [P, RING, T], F32)
        stats = sb("stats", [P, 2, 6], F32)
        moments = sb("moments", [P, 2, 2], F32)
        var_eps = sb("var_eps", [P, 2], F32)
        rstd = sb("rstd", [P, 2], F32)
        xnorm = sb("xnorm", [P, RING, T], F32)
        qk = sb("qk", [P, RING, 2, T], F32)
        qk_swap = sb("qk_swap", [P, RING, 2, T], F32)
        qk_rot = sb("qk_rot", [P, RING, 2, T], F32)
        rot_sin = sb("rot_sin", [P, 2, T], F32)
        values = sb("values", [P, RING, TT, G, 32], F32)
        rest = sb("rest", [P, 2, T], F32)
        parts = sb("parts", [P, RING, 2, PARTS, T], BF16)
        q_rows = sb("q_rows", [P, RING, G, T], BF16)
        k_rows = sb("k_rows", [P, RING, G, T], BF16)
        maxima = sb("maxima", [P, TT, G], F32)
        max_rest = sb("max_rest", [P, TT, HEADS], F32)
        max_parts = sb("max_parts", [P, 2, TT, PARTS, HEADS], BF16)
        max_rows = sb("max_rows", [PARTS * HEADS, 2, T], BF16)
        probs = sb("probs", [P, G, TT, T], F32)
        raw = sb("raw", [P, 2, T], F32)
        inv_sums = sb("inv_sums", [P, TT * HEADS], F32)
        by_target = sb("by_target", [P, TT, 2, C], F32)
        attended = sb("attended", [P, T], F32)
        xres = sb("xres", [P, RING, T], F32)
        x2 = sb("x2", [P, RING, T], F32)
        x2norm = sb("x2norm", [P, T], F32)
        x2hi = sb("x2hi", [P, TT, P], F16)
        x2lo = sb("x2lo", [P, TT, P], F16)
        hid = sb("hid", [P, HT * P], F32)
        hid_sq = sb("hid_sq", [P, HT * P], F32)
        hid_hi = sb("hid_hi", [P, HT * P], F16)
        hid_lo = sb("hid_lo", [P, HT * P], F16)
        xout = sb("xout", [P, RING, T], F32)

        max_ps = psum("max_ps", [P, 2, TT, T], F32)
        exp_ps = psum("exp_ps", [P, RING, TT, T], F32)
        att_ps = psum("att_ps", [P, 2 * T], F32)
        small_ps = psum("small_ps", [P, 2, 2 * T], F32)

        def small(user):
            which = [user in dict(users) for users in SMALL].index(True)
            return small_ps[:, which, 0:T]

        s_early = sem("project_consts_loaded")
        s_const = sem("const_loaded")
        s_wload = sem("ffn_weights_loaded")
        s_fill = sem("constants_filled")
        s_ones = sem("ones_made")
        s_rowones = sem("k_rows_filled")
        s_columns = sem("values_filled")
        s_id16 = sem("ident16_made")
        s_prep = sem("prep_step")
        s_wred = sem("weight_sums")
        s_wtot = sem("weight_totals")

        s_xin = [sem(f"x_loaded{u}") for u in range(RING)]
        s_cin = [sem(f"ctx_loaded{u}") for u in range(RING)]
        s_xres = [sem(f"xres_loaded{u}") for u in range(RING)]
        s_swap = [sem(f"swapped{u}") for u in range(RING)]
        s_wrote = [sem(f"parts_stored{u}") for u in range(RING)]
        s_seen = sem("parts_seen")
        s_rows = [sem(f"rows_loaded{u}") for u in range(RING)]
        s_mrow = [[sem(f"max_rows_loaded{b}{u}") for u in range(RING)] for b in range(2)]
        s_out = [sem(f"out_free{u}") for u in range(RING)]

        s_ln1 = sem("ln1_step")
        s_stats = sem("stats_seen")
        s_pow1 = sem("ln1_rstd")
        s_ln2 = sem("ln2_step")
        s_pow2 = sem("ln2_rstd")
        s_k = sem("k_made")
        s_v = sem("v_made")
        s_q = sem("q_made")
        s_kq = sem("kq_kept")
        s_vk = sem("v_kept")
        s_rot = sem("rotate_step")
        s_hi = sem("high_parts")
        s_rest = sem("rest_made")
        s_mid = sem("middle_parts")
        s_lo = sem("low_parts")
        s_sc = sem("max_scores_made")
        s_mx = sem("maxima_made")
        s_mc = sem("max_parts_step")
        s_mt = sem("max_turned")
        s_mk = sem("max_rows_kept")
        s_es = sem("exp_scores_made")
        s_ex = sem("probs_made")
        s_pv = sem("attended_made")
        s_raw = sem("raw_kept")
        s_at = sem("raw_turned")
        s_nm = sem("normalise_step")
        s_bk = sem("attended_turned")
        s_ak = sem("attended_kept")
        s_wo = sem("wo_made")
        s_xt = sem("x2_turned")
        s_xh = sem("x2_high")
        s_xl = sem("x2_low")
        s_hd = sem("hidden_made")
        s_hr = sem("hidden_kept")
        s_hh = sem("hidden_high")
        s_h2 = sem("hidden_squared")
        s_hl = sem("hidden_low")
        s_f2 = sem("ffn2_made")
        s_fin = sem("xout_made")

        def hidden_bank(n, i):
            return exp_ps[:, i, 0, :] if no_heads_after(n) else small(f"hid{i}")

        taken = {"max0": (s_mk, 2, 1), "max1": (s_mk, 2, 2), "xT": (s_xl, 1, 1), "v": (s_vk, 2, 2),
                 "att0": (s_nm, 6, 3), "att1": (s_nm, 6, 6), "back": (s_ak, 1, 1), "wo": (s_ln2, 5, 1),
                 "k": (s_kq, 2, 1), "q": (s_kq, 2, 2), "hid0": (s_hr, 3, 1), "hid1": (s_hr, 3, 2),
                 "hid2": (s_hr, 3, 3), "ffn2": (s_fin, 1, 1)}

        block = ctx.enter_context(nc.Block())

        def times_cos(engine, n):
            engine.wait_ge(s_early, 16 * 6)
            engine.wait_ge(s_kq, n.times(2, 2))
            engine.tensor_tensor(qk_rot[:, n.slot, :, :], qk[:, n.slot, :, :],
                                 cos[:].unsqueeze(1).broadcast_to([P, 2, T]), ALU.mult).then_inc(s_rot, 1)

        def plus_swapped_times_sin(engine, n):
            engine.wait_ge(s_swap[n.slot], n.turns(32))
            engine.tensor_tensor(rot_sin[:], qk_swap[:, n.slot, :, :],
                                 sin[:].unsqueeze(1).broadcast_to([P, 2, T]), ALU.mult).then_inc(s_rot, 1)
            engine.wait_ge(s_rot, n.times(3, 2))
            engine.tensor_tensor(qk_rot[:, n.slot, :, :], qk_rot[:, n.slot, :, :], rot_sin[:], ALU.add)\
                .then_inc(s_rot, 1)

        def rest_of(engine, n):
            engine.wait_ge(s_hi, n.times(1, 1))
            engine.tensor_tensor(rest[:], qk_rot[:, n.slot, :, :], parts[:, n.slot, :, 0, :], ALU.subtract)\
                .then_inc(s_rest, 1)

        def low_part_of(engine, n):
            engine.wait_ge(s_rest, n.times(1, 1))
            engine.wait_ge(s_mid, n.times(1, 1))
            engine.tensor_tensor(parts[:, n.slot, :, 2, :], rest[:], parts[:, n.slot, :, 1, :], ALU.subtract)\
                .then_inc(s_lo, 1)

        @block.sync
        def _(sp):
            def rows(dram, n):
                first = n.times(P, 0)
                if isinstance(first, int):
                    return dram[first:first + P, :]
                return dram[bass.ds(sp.snap(first), P), :]

            def load_x(n):
                if n.real:
                    x_rows = rows(x, n)
                    if not isinstance(n.j, int) or n.c >= RING:
                        sp.wait_ge(s_ln1, n.back(RING).times(4, 4))
                    sp.dma_start(xin[:, n.slot, :], x_rows).then_inc(s_xin[n.slot], 16)

            def load_ctx(n):
                if n.real:
                    ctx_rows = rows(ctx_in, n)
                    if not isinstance(n.j, int) or n.c >= RING:
                        sp.wait_ge(s_v, n.back(RING).times(1, 1))
                    sp.dma_start(cin[:, n.slot, :], ctx_rows).then_inc(s_cin[n.slot], 16)

            for u in range(RING):
                sp.sem_inc(s_out[u], 16)
            load_x(Count(0, 0))
            load_ctx(Count(0, 0))
            for dst, src in ((wq[:], wq_bd), (bq[:], bq_col), (wk[:], wk_bd), (bk[:], bk_col),
                             (cos[:], cos_t), (sin[:], sin_t)):
                sp.dma_start(dst, src).then_inc(s_early, 16)
            load_x(Count(0, 1))
            load_ctx(Count(0, 1))
            sp.dma_start(wfc[:], wfc_t).then_inc(s_wload, 16)
            sp.dma_start(wproj[:], wproj_t).then_inc(s_wload, 16)

            def load_late():
                sp.wait_ge(s_fill, 2)
                sp.dma_start(k_rows[ROWS:MROWS, :, :, :].rearrange("p u g t -> p (u g) t"),
                             ones16[0:PARTS, :].unsqueeze(1).broadcast_to([PARTS, RING * G, T])).then_inc(s_rowones, 16)
                for dst, src in ((wv[:], wv_bd), (ident[:], ident_t), (wo[:], wo_bd), (bv[:], bv_col),
                                 (bo[:], bo_col)):
                    sp.dma_start(dst, src).then_inc(s_const, 16)

            def store_maxima(n, b):
                if not n.real:
                    return
                u = n.slot
                sp.wait_ge(s_mk, n.times(2, 1 + b))
                sp.dma_start(q_rows[ROWS:MROWS, u, b * HEADS:(b + 1) * HEADS, :],
                             max_rows[:, b, :]).then_inc(s_mrow[b][u], 16)

            def step(s):
                if not is_first(s):
                    load_x(s.back(-1))
                store_maxima(s.back(3), 1)
                n = split = s.back(1)
                if n.real:
                    u = n.slot
                    sp.wait_ge(s_lo, n.times(1, 1))
                    sp.wait_ge(s_mid, n.times(1, 1))
                    sp.dma_start(spread[u].rearrange("a p r t -> r (a p) t"),
                                 parts[:, u, :, :, :].rearrange("r a p t -> r (a p) t")).then_inc(s_wrote[u], 16)
                n = s
                if n.real:
                    sp.wait_ge(s_kq, n.times(2, 2))
                    for half in range(2):
                        sp.dma_start(qk_swap[64 * half:64 * half + 64, n.slot, :, :],
                                     qk[64 - 64 * half:128 - 64 * half, n.slot, :, :]).then_inc(s_swap[n.slot], 16)
                if is_first(s):
                    load_late()
                else:
                    load_ctx(s.back(-1))
                n = s.back(3)
                if n.real:
                    x_rows = rows(x, n)
                    if not isinstance(n.j, int) or n.c >= RING:
                        sp.wait_ge(s_ln2, n.back(RING).times(5, 1))
                    sp.dma_start(xres[:, n.slot, :], x_rows).then_inc(s_xres[n.slot], 16)
                n = split
                if n.real:
                    u = n.slot
                    sp.wait_ge(s_wrote[u], n.turns(16))
                    sp.sem_inc(s_seen, 1)
                    if not isinstance(n.j, int) or n.c >= RING:
                        sp.wait_ge(s_es, n.back(RING).times(G, G))
                    else:
                        sp.wait_ge(s_rowones, 16)
                    for r in range(PARTS):
                        sp.dma_start(
                            q_rows[r * 24:r * 24 + 24, u, :, :],
                            spread[u, 0, r].rearrange("(c g) t -> c (g t)", g=G).unsqueeze(0)
                            .broadcast_to([PARTS, KC, G * T])).then_inc(s_rows[u], 16)
                    sp.dma_start(
                        k_rows[0:ROWS, u, :, :],
                        spread[u, 1].rearrange("p (c g) t -> (p c) (g t)", g=G).unsqueeze(0)
                        .broadcast_to([PARTS, PARTS * KC, G * T])).then_inc(s_rows[u], 16)
                n = s.back(6)
                if n.real:
                    out_rows = rows(out, n)
                    sp.wait_ge(s_fin, n.times(1, 1))
                    sp.dma_start(out_rows, xout[:, n.slot, :]).then_inc(s_out[n.slot], 16)
                store_maxima(s.back(2), 0)

            run_steps(sp, step)
            for u in range(RING):
                sp.wait_ge(s_out[u], 16 + 16 * len(range(u, PAIRS, RING)))

        @block.gpsimd
        def _(pool):
            pool.memset(minus_half[:], -0.5).then_inc(s_fill, 1)
            pool.memset(ones16[:], 1.0).then_inc(s_fill, 1)

            def fill_values(u):
                pool.memset(values[:, u, :, :, :], 0.0).then_inc(s_columns, 1)
                pool.wait_ge(s_columns, 3 * u + 1)
                by_head = values[:, u, :, :, :].rearrange("p t (j o) c -> p (t j) o c", o=2)
                pool.memset(by_head[:, :, 0, 16:24], 1.0).then_inc(s_columns, 1)
                pool.memset(by_head[:, :, 1, 24:32], 1.0).then_inc(s_columns, 1)

            def rstd_of(n, at, done, k, more, made):
                if n.real:
                    pool.wait_ge(done, n.times(k, more))
                    pool.tensor_tensor(rstd[:, at:at + 1], var_eps[:, at:at + 1], minus_half[:], ALU.pow)\
                        .then_inc(made, 1)

            def step(s):
                n = s.back(1)
                if n.real and not is_first(n):
                    rest_of(pool, n)
                    low_part_of(pool, n)
                n = s
                if n.real and not is_first(n):
                    times_cos(pool, n)
                rstd_of(s.back(-1), 0, s_ln1, 4, 3, s_pow1)
                if n.real and not is_first(n):
                    plus_swapped_times_sin(pool, n)
                if isinstance(s.j, int) and s.c < RING:
                    fill_values(s.c)
                n = s.back(5)
                if n.real and not is_last(n):
                    pool.wait_ge(s_hr, n.times(3, 3))
                    pool.tensor_tensor(hid_sq[:], hid[:], hid[:], ALU.mult).then_inc(s_h2, 1)
                    pool.wait_ge(s_h2, n.times(1, 1))
                    pool.wait_ge(s_hh, n.times(1, 1))
                    if not isinstance(n.j, int) or n.c >= 1:
                        pool.wait_ge(s_f2, n.times(1, 0))
                    pool.tensor_tensor(hid_lo[:], hid_sq[:], hid_hi[:], ALU.subtract).then_inc(s_hl, 1)
                rstd_of(s.back(4), 1, s_ln2, 5, 4, s_pow2)

            pool.wait_ge(s_fill, 1)
            rstd_of(Count(0, 0), 0, s_ln1, 4, 3, s_pow1)
            run_steps(pool, step)

        @block.scalar
        def _(act):
            act.wait_ge(s_fill, 2)
            act.activation(ones[:], ones16[:, 0:P], ACT.Copy).then_inc(s_ones, 1)
            act.wait_ge(s_early, 16 * 6)

            def keep_kq(n, which, made, user):
                if n.real:
                    src = small(user)
                    act.wait_ge(made, n.times(1, 1))
                    if which == 1 and (not isinstance(n.j, int) or n.c >= RING):
                        act.wait_ge(s_rot, n.back(RING).times(3, 3))
                    act.activation(qk[:, n.slot, which, :], src, ACT.Identity,
                                   bias=(bk if which else bq)[:, 0:1]).then_inc(s_kq, 1)

            def keep_v(n):
                if n.real:
                    if isinstance(n.j, int) and n.c == 0:
                        act.wait_ge(s_const, 16 * 5)
                        act.activation(ident16[:], ident[:], ACT.Copy).then_inc(s_id16, 1)
                    src = small("v")
                    act.wait_ge(s_v, n.times(1, 1))
                    if not isinstance(n.j, int) or n.c >= RING:
                        act.wait_ge(s_pv, n.back(RING).times(8, 8))
                    else:
                        act.wait_ge(s_columns, 3 + 3 * n.slot)
                    dst = values[:, n.slot, :, :, :].rearrange("p t g c -> p (t g c)")
                    for o in range(2):
                        act.activation(
                            dst.rearrange("p (m o c) -> p m o c", o=2, c=32)[:, :, o, 8 * o:8 * o + 8],
                            src.rearrange("p (m o c) -> p m o c", o=2, c=8)[:, :, o, :], ACT.Copy)\
                            .then_inc(s_vk, 1)

            def keep_max(n, b):
                if n.real:
                    src = small(f"max{b}")
                    act.wait_ge(s_mt, n.times(2, 1 + b))
                    if not isinstance(n.j, int) or n.c >= 1:
                        act.wait_ge(s_mrow[b][n.back(1).slot], n.back(1).turns(16))
                    turned = src[:, 0:P].bitcast(BF16)
                    act.activation(max_rows[:, b, :], turned[0:PARTS * HEADS, :], ACT.Copy).then_inc(s_mk, 1)

            def keep_raw(n, b):
                if n.real:
                    act.wait_ge(s_pv, n.times(8, 4 * b + 4))
                    if not isinstance(n.j, int) or n.c >= 1:
                        act.wait_ge(s_at, n.times(2, b - 1))
                    act.activation(raw[:, b, :], att_ps[:, 0:T], ACT.Copy).then_inc(s_raw, 1)

            def keep_attended(n):
                if n.real:
                    src = small("back")
                    act.wait_ge(s_bk, n.times(1, 1))
                    if not isinstance(n.j, int) or n.c >= 1:
                        act.wait_ge(s_wo, n.times(1, 0))
                    act.activation(attended[:], src, ACT.Copy).then_inc(s_ak, 1)

            def exp(n, k):
                if n.real:
                    act.wait_ge(s_es, n.times(G, k + 1))
                    if not isinstance(n.j, int) or n.c >= 1:
                        act.wait_ge(s_pv, n.times(8, -8 + 2 * (k // 4) + 2))
                    act.activation(probs[:, k, :, :], exp_ps[:, (n.slot + k) % RING, :, :], ACT.Exp, scale=SCALE)\
                        .then_inc(s_ex, 1)

            def high(n):
                if n.real:
                    act.wait_ge(s_rot, n.times(3, 3))
                    if not isinstance(n.j, int) or n.c >= RING:
                        act.wait_ge(s_wrote[n.slot], n.turns(16, -16))
                    act.activation(parts[:, n.slot, :, 0, :], qk_rot[:, n.slot, :, :], ACT.Copy).then_inc(s_hi, 1)

            def middle(n):
                if n.real:
                    act.wait_ge(s_rest, n.times(1, 1))
                    act.activation(parts[:, n.slot, :, 1, :], rest[:], ACT.Copy).then_inc(s_mid, 1)

            def relu(n, i):
                if n.real:
                    src = hidden_bank(n, i)
                    act.wait_ge(s_hd, n.times(3, i + 1))
                    if i == 0 and (not isinstance(n.j, int) or n.c >= 1):
                        act.wait_ge(s_h2, n.times(1, 0))
                        act.wait_ge(s_hh, n.times(1, 0))
                    cols = T if i < 2 else P
                    act.activation(hid[:, i * T:i * T + cols], src[:, 0:cols], ACT.Relu,
                                   scale=RELU_SCALE).then_inc(s_hr, 1)

            def square(n):
                if n.real:
                    act.wait_ge(s_hr, n.times(3, 3))
                    if not isinstance(n.j, int) or n.c >= 1:
                        act.wait_ge(s_f2, n.times(1, 0))
                        act.wait_ge(s_hl, n.times(1, 0))
                    act.activation(hid_hi[:], hid[:], ACT.Square).then_inc(s_hh, 1)

            def x2_high(n):
                if n.real:
                    src = small("xT")
                    act.wait_ge(s_xt, n.times(1, 1))
                    if not isinstance(n.j, int) or n.c >= 1:
                        act.wait_ge(s_hd, n.times(3, 0))
                    act.activation(x2hi[:].rearrange("p a b -> p (a b)"), src, ACT.Copy).then_inc(s_xh, 1)

            def step(s):
                maxima_of, attending, ending = s.back(2), s.back(3), s.back(4)
                high(s.back(1))
                turn_at = 5 if s.back(3).real else 1
                for k in range(G):
                    exp(attending, k)
                    if k == turn_at:
                        x2_high(s.back(5))
                    if k == 1:
                        middle(s.back(1))
                        keep_v(maxima_of)
                    if k == 2:
                        keep_kq(s, 1, s_k, "k")
                    if k == 3:
                        keep_max(attending, 1)
                    if k == 4:
                        keep_raw(ending, 1)
                        keep_kq(s, 0, s_q, "q")
                    if k == 7:
                        relu(s.back(5), 0)
                    if k == 9:
                        relu(s.back(5), 1)
                    if k == 10:
                        keep_attended(ending)
                        relu(s.back(5), 2)
                        square(s.back(5))
                    if k == 11:
                        keep_raw(attending, 0)
                    if k == 12:
                        keep_max(maxima_of, 0)

            run_steps(act, step)

        @block.vector
        def _(dve):
            def stats_of(src, at, done):
                dve.bn_stats(stats[:, at, :], src).then_inc(done, 1)

            def moments_of(n, at, done, k, first):
                dve.wait_ge(done, n.times(k, first + 1))
                dve.sem_inc(s_stats, 1)
                dve.bn_aggr(moments[:, at, :], stats[:, at, :]).then_inc(done, 1)

            def var_eps_of(n, at, done, k, first):
                dve.wait_ge(done, n.times(k, first + 2))
                dve.tensor_scalar(var_eps[:, at:at + 1], moments[:, at, 1:2], EPS, None, ALU.add)\
                    .then_inc(done, 1)

            def normalised(n, src, at, dst, done, made):
                dve.wait_ge(made, n.times(1, 1))
                dve.tensor_scalar(dst, src, moments[:, at, 0:1], rstd[:, at:at + 1], ALU.subtract, ALU.mult)\
                    .then_inc(done, 1)

            def ln1(n, i):
                if n.real:
                    if i == 0:
                        dve.wait_ge(s_xin[n.slot], n.turns(16))
                        stats_of(xin[:, n.slot, :], 0, s_ln1)
                    if i == 1:
                        moments_of(n, 0, s_ln1, 4, 0)
                    if i == 2:
                        var_eps_of(n, 0, s_ln1, 4, 0)
                    if i == 3:
                        if not isinstance(n.j, int) or n.c >= RING:
                            dve.wait_ge(s_q, n.back(RING).times(1, 1))
                        normalised(n, xin[:, n.slot, :], 0, xnorm[:, n.slot, :], s_ln1, s_pow1)

            def ln2(n, i):
                if n.real:
                    u = n.slot
                    if i == 0:
                        src = small("wo")
                        dve.wait_ge(s_wo, n.times(1, 1))
                        dve.wait_ge(s_xres[u], n.turns(16))
                        dve.scalar_tensor_tensor(out=x2[:, u, :], in0=src, scalar=out_bias[:, 0:1],
                                                 in1=xres[:, u, :], op0=ALU.add, op1=ALU.add).then_inc(s_ln2, 1)
                    if i == 1:
                        dve.wait_ge(s_ln2, n.times(5, 1))
                        stats_of(x2[:, u, :], 1, s_ln2)
                    if i == 2:
                        moments_of(n, 1, s_ln2, 5, 1)
                    if i == 3:
                        var_eps_of(n, 1, s_ln2, 5, 1)
                    if i == 4:
                        if not isinstance(n.j, int) or n.c >= 1:
                            dve.wait_ge(s_xt, n.times(1, 0))
                        normalised(n, x2[:, u, :], 1, x2norm[:], s_ln2, s_pow2)

            def x2_low(n):
                if n.real:
                    src = small("xT")
                    dve.wait_ge(s_xh, n.times(1, 1))
                    if not isinstance(n.j, int) or n.c >= 1:
                        dve.wait_ge(s_hd, n.times(3, 0))
                    dve.tensor_tensor(x2lo[:].rearrange("p a b -> p (a b)"), src,
                                      x2hi[:].rearrange("p a b -> p (a b)"), ALU.subtract).then_inc(s_xl, 1)

            def head_max(n, k):
                if n.real:
                    g = k // HEADS * HEADS + ORDER[k % HEADS]
                    dve.wait_ge(s_sc, n.times(G, k + 1))
                    dve.tensor_reduce(maxima[:, :, g], max_ps[:, k % 2, :, :], AX_X, ALU.max).then_inc(s_mx, 1)

            def split_max(n, b, i):
                if n.real:
                    m = maxima[:, :, b * HEADS:(b + 1) * HEADS]
                    part = [max_parts[:, b, :, p, :] for p in range(PARTS)]
                    if i:
                        dve.wait_ge(s_mc, n.times(8, 4 * b + i))
                    if i == 0:
                        dve.wait_ge(s_mx, n.times(G, (b + 1) * HEADS))
                        if not isinstance(n.j, int) or n.c >= 1:
                            dve.wait_ge(s_mt, n.times(2, b - 1))
                        dve.tensor_scalar(part[0], m, -1.0, None, ALU.mult).then_inc(s_mc, 1)
                    if i == 1:
                        dve.scalar_tensor_tensor(out=max_rest[:], in0=m, scalar=-1.0, in1=part[0], op0=ALU.mult,
                                                 op1=ALU.subtract).then_inc(s_mc, 1)
                    if i == 2:
                        dve.tensor_copy(part[1], max_rest[:]).then_inc(s_mc, 1)
                    if i == 3:
                        dve.tensor_tensor(part[2], max_rest[:], part[1], ALU.subtract).then_inc(s_mc, 1)

            def invert(n, b):
                if n.real:
                    heads = small(f"att{b}").rearrange("p (m o c) -> p m o c", o=4, c=KC)
                    dve.wait_ge(s_at, n.times(2, b + 1))
                    dve.reciprocal(inv_sums[:].rearrange("p (m o) -> p m o", o=2), heads[:, :, 2:4, 0])\
                        .then_inc(s_nm, 1)

            def divide(n, b):
                if n.real:
                    src = small(f"att{b}")
                    heads = src.rearrange("p (m o c) -> p m o c", o=4, c=KC)
                    dve.wait_ge(s_nm, n.times(6, 3 * b + 1))
                    if not isinstance(n.j, int) or n.c >= 1:
                        dve.wait_ge(s_bk, n.times(1, 0))
                    half_heads = HEADS // 2
                    for t in range(TT):
                        at = slice(t * half_heads, (t + 1) * half_heads)
                        dve.tensor_tensor(
                            by_target[:, t, b, :].rearrange("p (j o c) -> p j o c", o=2, c=KC),
                            heads[:, at, 0:2, :],
                            inv_sums[:].rearrange("p (m o) -> p m o", o=2)[:, at, :].unsqueeze(3)
                            .broadcast_to([P, half_heads, 2, KC]), ALU.mult).then_inc(s_nm, 1)

            def finish(n):
                if n.real:
                    u = n.slot
                    src = small("ffn2")
                    dve.wait_ge(s_f2, n.times(1, 1))
                    dve.wait_ge(s_out[u], n.turns(16))
                    dve.scalar_tensor_tensor(out=xout[:, u, :], in0=src, scalar=fscale[:, 1:2], in1=x2[:, u, :],
                                             op0=ALU.mult, op1=ALU.add).then_inc(s_fin, 1)

            def hidden_low(n):
                dve.wait_ge(s_hr, n.times(3, 3))
                dve.tensor_tensor(hid_sq[:], hid[:], hid[:], ALU.mult).then_inc(s_h2, 1)
                dve.wait_ge(s_h2, n.times(1, 1))
                dve.wait_ge(s_hh, n.times(1, 1))
                dve.wait_ge(s_f2, n.times(1, 0))
                dve.tensor_tensor(hid_lo[:], hid_sq[:], hid_hi[:], ALU.subtract).then_inc(s_hl, 1)

            def prepare_sums():
                dve.wait_ge(s_wload, 32)
                dve.tensor_reduce(wsum[:, 0:1], wfc[:].rearrange("p a b -> p (a b)"), AX_X, ALU.add,
                                  apply_absolute_value=True).then_inc(s_wred, 1)
                dve.tensor_reduce(wsum[:, 1:2], wproj[:].rearrange("p a b -> p (a b)"), AX_X, ALU.add,
                                  apply_absolute_value=True).then_inc(s_wred, 1)

            def prepare_means():
                dve.wait_ge(s_wtot, 1)
                dve.wait_ge(s_const, 16 * 5)
                dve.tensor_scalar(out_bias[:], att_ps[:, 4:5], bo[:, 0:1], None, ALU.add).then_inc(s_prep, 1)
                dve.tensor_scalar(wmean[:], att_ps[:, 0:2], 1.0 / (HID * T), 1e-5, ALU.mult, ALU.max)\
                    .then_inc(s_prep, 1)
                dve.wait_ge(s_prep, 2)
                dve.tensor_scalar(wthr[:], wmean[:], 0.7, None, ALU.mult).then_inc(s_prep, 1)
                dve.tensor_scalar(wnthr[:], wmean[:], -0.7, None, ALU.mult).then_inc(s_prep, 1)
                dve.tensor_tensor(fscale[:, 0:1], wmean[:, 0:1], wmean[:, 0:1], ALU.mult).then_inc(s_prep, 1)
                dve.wait_ge(s_prep, 5)
                dve.tensor_scalar(fscale[:, 1:2], fscale[:, 0:1], wmean[:, 1:2], RELU_SCALE ** -2,
                                  ALU.mult, ALU.mult).then_inc(s_prep, 1)

            def make_ternary(i):
                w, w3 = ((wfc, fc3), (wproj, proj3))[i]
                flat, flat3 = (t[:].rearrange("p a b -> p (a b)") for t in (w, w3))
                dve.wait_ge(s_prep, 6 + 2 * i)
                dve.tensor_scalar(below[:], flat, wnthr[:, i:i + 1], None, ALU.is_lt).then_inc(s_prep, 1)
                dve.wait_ge(s_prep, 7 + 2 * i)
                dve.scalar_tensor_tensor(out=flat3, in0=flat, scalar=wthr[:, i:i + 1], in1=below[:],
                                         op0=ALU.is_gt, op1=ALU.subtract).then_inc(s_prep, 1)

            def step(s):
                maxima_of, attending, ending = s.back(2), s.back(3), s.back(4)
                if isinstance(s.j, int) and s.c == 1:
                    rest_of(dve, s.back(1))
                    low_part_of(dve, s.back(1))
                    prepare_sums()
                split_max(attending, 1, 0)
                split_max(attending, 1, 1)
                split_max(attending, 1, 2)
                for k in range(G):
                    head_max(maxima_of, k)
                    if k == 0:
                        split_max(attending, 1, 3)
                        if attending.real:
                            finish(s.back(6))
                    if k == 1:
                        ln2(s.back(5), 4)
                    if k == 5:
                        x2_low(s.back(5))
                        if not attending.real:
                            finish(s.back(6))
                    if k in (1, 2, 3):
                        ln1(s.back(-1), k - 1)
                    if k == 7:
                        if is_last(s.back(5)):
                            hidden_low(s.back(5))
                        invert(ending, 1)
                    if k == 8:
                        divide(ending, 1)
                        split_max(maxima_of, 0, 0)
                    if k == 9:
                        split_max(maxima_of, 0, 1)
                    if k == 10:
                        split_max(maxima_of, 0, 2)
                        split_max(maxima_of, 0, 3)
                    if k in (12, 13, 14, 15):
                        ln2(ending, k - 12)
                    if k == 9:
                        ln1(s.back(-1), 3)
                        if isinstance(s.j, int) and s.c == 1:
                            prepare_means()
                            for i in range(2):
                                make_ternary(i)
                    if k == 14:
                        invert(attending, 0)
                divide(attending, 0)
                if is_first(s):
                    times_cos(dve, s)
                    plus_swapped_times_sin(dve, s)

            for i in range(4):
                ln1(Count(0, 0), i)
            run_steps(dve, step)

        @block.tensor
        def _(pe):
            def claim(user, s):
                before = user_before(user, s)
                if before:
                    user_left, n = before
                    done, for_a_pair, at = taken[user_left]
                    pe.wait_ge(done, n.times(for_a_pair, at))
                return small(user)

            def make_k(s):
                if s.real:
                    dst = claim("k", s)
                    pe.wait_ge(s_cin[s.slot], s.turns(16))
                    pe.matmul(dst, wk[:], cin[:, s.slot, :], start=True, stop=True).then_inc(s_k, 1)

            def make_v(n, s):
                if n.real:
                    dst = claim("v", s)
                    for t in range(TT):
                        mm = pe.matmul(dst[:, t * P:(t + 1) * P], cin[:, n.slot, t * P:(t + 1) * P], wv[:],
                                       start=True, stop=True)
                    mm.then_inc(s_v, 1)

            def make_q(s):
                if s.real:
                    dst = claim("q", s)
                    pe.wait_ge(s_ln1, s.times(4, 4))
                    pe.matmul(dst, wq[:], xnorm[:, s.slot, :], start=True, stop=True).then_inc(s_q, 1)

            def turn_max(n, b, s):
                if n.real:
                    turned = claim(f"max{b}", s)[:, 0:P].bitcast(BF16)
                    if isinstance(n.j, int) and n.c == 0:
                        pe.wait_ge(s_id16, 1)
                    pe.wait_ge(s_mc, n.times(8, 4 * b + 4))
                    for t in range(TT):
                        mm = pe.transpose(turned[0:PARTS * HEADS, t * P:(t + 1) * P],
                                          max_parts[:, b, t, :, :].rearrange("p a h -> p (a h)"), ident16[:])
                    mm.then_inc(s_mt, 1)

            def max_scores(n, k):
                if n.real:
                    u, g = n.slot, k // HEADS * HEADS + ORDER[k % HEADS]
                    if k == 0:
                        pe.wait_ge(s_rows[u], n.turns(64))
                    if k >= 2 or not isinstance(n.j, int) or n.c >= 1:
                        pe.wait_ge(s_mx, n.times(G, k - 1))
                    for t in range(TT):
                        mm = pe.matmul(max_ps[:, k % 2, t, :], q_rows[0:ROWS, u, g, t * P:(t + 1) * P],
                                       k_rows[0:ROWS, u, g, :], start=True, stop=True)
                    mm.then_inc(s_sc, 1)

            def exp_scores(n, k):
                if n.real:
                    u, g = n.slot, k // HEADS * HEADS + ORDER[k % HEADS]
                    if k % HEADS == 0:
                        pe.wait_ge(s_mrow[k // HEADS][u], n.turns(16))
                    if k >= RING or not isinstance(n.j, int) or n.c >= 1:
                        pe.wait_ge(s_ex, n.times(G, k + 1 - RING))
                    for t in range(TT):
                        mm = pe.matmul(exp_ps[:, (u + k) % RING, t, :], k_rows[0:MROWS, u, g, t * P:(t + 1) * P],
                                       q_rows[0:MROWS, u, g, :], start=True, stop=True)
                    mm.then_inc(s_es, 1)

            def attend(n, part):
                if n.real:
                    quad, t = part // 2, part % 2
                    b, odd = quad // 2, quad % 2
                    if t == 0:
                        pe.wait_ge(s_ex, n.times(G, 4 * quad + 4))
                    if part == 0:
                        pe.wait_ge(s_vk, n.times(2, 2))
                        if isinstance(n.j, int) and n.c == 0:
                            pe.wait_ge(s_prep, 2)
                    if part == 4 or part == 0 and (not isinstance(n.j, int) or n.c >= 1):
                        pe.wait_ge(s_raw, n.times(2, b))
                    for j in range(4):
                        mm = pe.matmul(att_ps[32 * j:32 * j + 32, 0:T],
                                       values[:, n.slot, t, b * HEADS + 2 * j + odd, :],
                                       probs[:, 4 * quad + j, t, :],
                                       start=(part % 4 == 0), stop=(part % 4 == 3))
                    mm.then_inc(s_pv, 1)

            def turn(dst, parts_in, done):
                for t in range(TT):
                    mm = pe.transpose(dst[:, t * P:(t + 1) * P], parts_in[t], ident[:])
                mm.then_inc(done, 1)

            def turn_raw(n, b, s):
                if n.real:
                    dst = claim(f"att{b}", s)
                    pe.wait_ge(s_raw, n.times(2, b + 1))
                    turn(dst, [raw[:, b, t * P:(t + 1) * P] for t in range(TT)], s_at)

            def turn_back(n, s):
                if n.real:
                    dst = claim("back", s)
                    pe.wait_ge(s_nm, n.times(6, 6))
                    turn(dst, [by_target[:, t, :, :].rearrange("p b c -> p (b c)") for t in range(TT)], s_bk)

            def project_out(n, s):
                if n.real:
                    dst = claim("wo", s)
                    pe.wait_ge(s_ak, n.times(1, 1))
                    pe.matmul(dst, wo[:], attended[:], start=True, stop=True).then_inc(s_wo, 1)

            def turn_x2(n, s):
                if n.real:
                    dst = claim("xT", s)
                    pe.wait_ge(s_ln2, n.times(5, 5))
                    turn(dst, [x2norm[:, t * P:(t + 1) * P] for t in range(TT)], s_xt)

            def hidden(n, i, s):
                if n.real:
                    if no_heads_after(n):
                        pe.wait_ge(s_ex, G * PAIRS)
                    else:
                        claim(f"hid{i}", s)
                    dst = hidden_bank(n, i)
                    if i == 0:
                        pe.wait_ge(s_xl, n.times(1, 1))
                        if isinstance(n.j, int) and n.c == 0:
                            pe.wait_ge(s_prep, 10)
                    for h in range(2 * i, min(2 * i + 2, HT)):
                        at = (h - 2 * i) * P
                        for m, (t, half) in enumerate((t, half) for half in (x2hi, x2lo) for t in range(TT)):
                            mm = pe.matmul(dst[:, at:at + P], fc3[:, t, h * P:(h + 1) * P],
                                           half[:, t, :], start=(m == 0), stop=(m == 3))
                    mm.then_inc(s_hd, 1)

            def ffn2(n, s):
                if n.real:
                    dst = claim("ffn2", s)
                    pe.wait_ge(s_hh, n.times(1, 1))
                    for m, (h, half) in enumerate((h, half) for half in (hid_hi, hid_lo) for h in range(HT)):
                        if m == HT:
                            pe.wait_ge(s_hl, n.times(1, 1))
                        mm = pe.matmul(dst, half[:, h * P:(h + 1) * P], proj3[:, h, :],
                                       start=(m == 0), stop=(m == 2 * HT - 1))
                    mm.then_inc(s_f2, 1)

            pe.wait_ge(s_early, 16 * 6)

            def totals():
                pe.wait_ge(s_const, 16 * 5)
                pe.wait_ge(s_ones, 1)
                pe.wait_ge(s_wred, 2)
                pe.matmul(att_ps[:, 0:2], ones[:], wsum[:], start=True, stop=True)
                pe.matmul(att_ps[:, 4:5], wo[:], bv[:], start=True, stop=True).then_inc(s_wtot, 1)

            def warm_clock():
                for i in range(CLOCK_WARM):
                    pe.matmul(exp_ps[:, 0, :, :].rearrange("p a b -> p (a b)"), ones[:],
                              wfc[:, 0, 0:2 * T], start=True, stop=True)

            def hold_clock():
                for i in range(CLOCK_HOLD):
                    for t in range(TT):
                        pe.matmul(exp_ps[:, i, t, :], q_rows[0:ROWS, 0, 0, 0:P], k_rows[0:ROWS, 0, 0, :],
                                  start=True, stop=True)

            def step(s):
                maxima_of, attending, ending, feeding = s.back(2), s.back(3), s.back(4), s.back(5)
                turn_at = 5 if s.back(3).real else 1
                for k in range(G):
                    if k in (0, 2, 4):
                        attend(ending, 5 + k // 2)
                    if k in (7, 8, 10, 11, 14):
                        attend(attending, (7, 8, 10, 11, 14).index(k))
                    exp_scores(attending, k)
                    max_scores(maxima_of, k)
                    if k == 1:
                        make_v(maxima_of, s)
                    if k == 2:
                        make_k(s)
                    if k == 3:
                        turn_max(attending, 1, s)
                    if k == 4:
                        make_q(s)
                        if isinstance(s.j, int) and s.c == 1:
                            totals()
                            warm_clock()
                    if isinstance(s.j, int) and s.c == 2:
                        hold_clock()
                    if k == turn_at:
                        turn_x2(feeding, s)
                    if k == 7:
                        hidden(feeding, 0, s)
                        turn_raw(ending, 1, s)
                    if k == 9:
                        hidden(feeding, 1, s)
                    if k == 10:
                        turn_back(ending, s)
                        hidden(feeding, 2, s)
                    if k == 12:
                        project_out(ending, s)
                        turn_max(maxima_of, 0, s)
                    if k == 14:
                        turn_raw(attending, 0, s)
                    if k == 15:
                        ffn2(feeding, s)

            run_steps(pe, step)


def kernel(x, ctx_2048, L0_xattn_Wq, L0_xattn_bq, L0_xattn_Wk, L0_xattn_bk, L0_xattn_Wv, L0_xattn_bv,
           L0_xattn_Wo, L0_xattn_bo, L0_ffn_w_fc, L0_ffn_w_proj):
    import numpy as np
    import concourse.bacc as bacc
    from concourse.bass_utils import run_bass_kernel_spmd

    def by_channel(w):
        t = np.zeros((2, C, KC, 2, HEADS), np.float32)
        for b in range(2):
            t[b, :, :, b, :] = np.asarray(w).reshape(HEADS, KC, C).transpose(2, 1, 0)
        return t.reshape(P, P)

    def bias_by_channel(v):
        t = np.zeros((KC, 2, HEADS), np.float32)
        for b in range(2):
            t[:, b, :] = np.asarray(v).reshape(HEADS, KC).transpose(1, 0)
        return t.reshape(P, 1)

    wv_bd = np.zeros((2, C, 2, C), np.float32)
    wo_bd = np.zeros((2, C, 2, C), np.float32)
    bo_col = np.zeros((2, C), np.float32)
    bv_col = np.zeros((2, C), np.float32)
    for b in range(2):
        wv_bd[b, :, b, :] = np.asarray(L0_xattn_Wv).T
        wo_bd[b, :, b, :] = np.asarray(L0_xattn_Wo).T
        bo_col[b] = np.asarray(L0_xattn_bo)
        bv_col[b] = np.asarray(L0_xattn_bv)

    inv = (1.0 / np.float32(10000.0) ** (np.arange(0, KC, 2, dtype=np.float32) / np.float32(KC))).astype(np.float32)
    angle = (np.arange(T, dtype=np.float32)[None, :] * np.tile(inv, 2)[:, None]).astype(np.float32)
    sign = np.repeat(np.array([-1.0, 1.0], np.float32), KC // 2)[:, None]
    cos_t = np.repeat(np.cos(angle), G, axis=0).astype(np.float32)
    sin_t = np.repeat(np.sin(angle) * sign, G, axis=0).astype(np.float32)

    arrays = {
        "x": np.asarray(x).reshape(BATCHES * C, T),
        "ctx_in": np.asarray(ctx_2048).reshape(BATCHES * C, T),
        "wq_bd": by_channel(L0_xattn_Wq), "wk_bd": by_channel(L0_xattn_Wk), "wv_bd": wv_bd.reshape(P, P),
        "wo_bd": wo_bd.reshape(P, P),
        "bq_col": bias_by_channel(L0_xattn_bq), "bk_col": bias_by_channel(L0_xattn_bk),
        "bv_col": bv_col.reshape(P, 1), "bo_col": bo_col.reshape(P, 1),
        "wfc_t": np.ascontiguousarray(np.asarray(L0_ffn_w_fc).T.reshape(TT, P, HID).transpose(1, 0, 2)),
        "wproj_t": np.ascontiguousarray(np.asarray(L0_ffn_w_proj).T.reshape(HT, P, T).transpose(1, 0, 2)),
        "cos_t": cos_t, "sin_t": sin_t, "ident_t": np.eye(P, dtype=np.float32),
    }
    nc = bacc.Bacc("TRN2", target_bir_lowering=False, num_devices=1)
    args = [nc.dram_tensor(f"in_{name}", a.shape, F32, kind="ExternalInput").ap() for name, a in arrays.items()]
    out = nc.dram_tensor("out_x", (BATCHES * C, T), F32, kind="ExternalOutput").ap()
    xattn_ffn(nc, *args, out)
    r = run_bass_kernel_spmd(nc, [{f"in_{name}": a for name, a in arrays.items()}], core_ids=[0])
    return r.results[0]["out_x"].reshape(BATCHES, C, T)
```
